# Optimizing a Trainium2 kernel written in Bass

```python
import numpy as np
import jax
import jax.numpy as jnp

def _softmax(x, axis=-1):
    return jax.nn.softmax(x, axis=axis)

def _gelu(x):
    return jax.nn.gelu(x, approximate=True)

def _silu(x):
    return jax.nn.silu(x)

def _sigmoid(x):
    return jax.nn.sigmoid(x)

def _layernorm(x, axis=-1, eps=1e-05):
    m = jnp.mean(x, axis=axis, keepdims=True)
    v = jnp.var(x, axis=axis, keepdims=True)
    return (x - m) / jnp.sqrt(v + eps)

def _scatter_add(tgt, idx, src, axis=0):
    return tgt.at[idx].add(src)

def _segment_sum(src, seg, n):
    return jax.ops.segment_sum(src, seg, n)
kernel_name = 'mk_sandwich_d1_jaxref_r8_c92947'

def setup_inputs(seed: int=0):
    np.random.seed(seed)
    _w = jnp.asarray

    def _L0_attn_setup():
        import jax, jax.numpy as jnp
        import numpy as np
        import math
        B, T, D = (4, 512, 256)
        H = 16
        HD = D // H
        L = 64
        K_TOP = 4
        key = jax.random.key(seed)
        ks = jax.random.split(key, 10)
        lim = 1.0 / math.sqrt(D)
        u = lambda k, shape: jax.random.uniform(k, shape, jnp.float32, -lim, lim)
        return {'hidden_states': jax.random.normal(ks[0], (B, T, D), jnp.float32), 'Wq': u(ks[1], (D, D)), 'bq': u(ks[2], (D,)), 'Wk': u(ks[3], (D, D)), 'bk': u(ks[4], (D,)), 'Wv': u(ks[5], (D, D)), 'bv': u(ks[6], (D,)), 'Wo': u(ks[7], (D, D)), 'bo': u(ks[8], (D,)), 'latent_keys': jax.random.normal(ks[9], (L, D), jnp.float32) * 0.1}
    _L0_attn_in = _L0_attn_setup()

    def _L0_ffn_setup():
        import jax, jax.numpy as jnp
        import numpy as np
        HIDDEN = 256
        INTER = 688
        LUT_SIZE = 16

        def _ghost_linear(x, idx, lut):
            w = lut[idx]
            return jnp.einsum('bsh,oh->bso', x, w)
        key = jax.random.key(seed)
        k_x, k_lut, k_g, k_u, k_d = jax.random.split(key, 5)
        x = jax.random.normal(k_x, (2, 512, HIDDEN), dtype=jnp.float32)
        lut = jax.random.normal(k_lut, (LUT_SIZE,), dtype=jnp.float32) * 0.02
        gate_idx = jax.random.randint(k_g, (INTER, HIDDEN), 0, LUT_SIZE, dtype=jnp.int32)
        up_idx = jax.random.randint(k_u, (INTER, HIDDEN), 0, LUT_SIZE, dtype=jnp.int32)
        down_idx = jax.random.randint(k_d, (HIDDEN, INTER), 0, LUT_SIZE, dtype=jnp.int32)
        return {'x': x, 'lut': lut, 'gate_idx': gate_idx, 'up_idx': up_idx, 'down_idx': down_idx}
    _L0_ffn_in = _L0_ffn_setup()
    _d = {'L0_attn_hidden_states': _L0_attn_in['hidden_states'], 'L0_attn_Wq': _L0_attn_in['Wq'], 'L0_attn_bq': _L0_attn_in['bq'], 'L0_attn_Wk': _L0_attn_in['Wk'], 'L0_attn_bk': _L0_attn_in['bk'], 'L0_attn_Wv': _L0_attn_in['Wv'], 'L0_attn_bv': _L0_attn_in['bv'], 'L0_attn_Wo': _L0_attn_in['Wo'], 'L0_attn_bo': _L0_attn_in['bo'], 'L0_attn_latent_keys': _L0_attn_in['latent_keys'], 'L0_ffn_lut': _L0_ffn_in['lut'], 'L0_ffn_gate_idx': _L0_ffn_in['gate_idx'], 'L0_ffn_up_idx': _L0_ffn_in['up_idx'], 'L0_ffn_down_idx': _L0_ffn_in['down_idx']}
    _x0 = _d['L0_attn_hidden_states']
    _d['L0_attn_hidden_states'] = jax.random.normal(jax.random.fold_in(jax.random.key(seed), 1), (1, 2048, 256), dtype=_x0.dtype)
    del _x0
    return _d

def reference(L0_attn_hidden_states, L0_attn_Wq, L0_attn_bq, L0_attn_Wk, L0_attn_bk, L0_attn_Wv, L0_attn_bv, L0_attn_Wo, L0_attn_bo, L0_attn_latent_keys, L0_ffn_lut, L0_ffn_gate_idx, L0_ffn_up_idx, L0_ffn_down_idx):

    def _L0_attn_ref(hidden_states, Wq, bq, Wk, bk, Wv, bv, Wo, bo, latent_keys):
        import jax, jax.numpy as jnp
        import numpy as np
        import math
        B, T, D = (4, 512, 256)
        H = 16
        HD = D // H
        L = 64
        K_TOP = 4
        b, t, d = hidden_states.shape
        Q = (hidden_states @ Wq.T + bq).reshape(b, t, H, HD).transpose(0, 2, 1, 3)
        K = (hidden_states @ Wk.T + bk).reshape(b, t, H, HD).transpose(0, 2, 1, 3)
        V = (hidden_states @ Wv.T + bv).reshape(b, t, H, HD).transpose(0, 2, 1, 3)
        latent = latent_keys.reshape(L, H, HD)
        attn_logits = jnp.einsum('bhtd,lhd->bhtl', Q, latent) / math.sqrt(HD)
        topk_logits, topk_idx = jax.lax.top_k(attn_logits, K_TOP)
        attn_weights = jax.nn.softmax(topk_logits, axis=-1)
        latent_h = latent.transpose(1, 0, 2)
        selected = latent_h[jnp.arange(H)[None, :, None, None], topk_idx]
        weighted = jnp.einsum('bhtk,bhtkd->bhtd', attn_weights, selected)
        attn_output = (weighted + V).transpose(0, 2, 1, 3).reshape(b, t, d)
        return attn_output @ Wo.T + bo

    def _L0_ffn_ref(x, lut, gate_idx, up_idx, down_idx):
        import jax, jax.numpy as jnp
        import numpy as np
        HIDDEN = 256
        INTER = 688
        LUT_SIZE = 16

        def _ghost_linear(x, idx, lut):
            w = lut[idx]
            return jnp.einsum('bsh,oh->bso', x, w)
        gate = _ghost_linear(x, gate_idx, lut)
        up = _ghost_linear(x, up_idx, lut)
        h = jax.nn.silu(gate) * up
        return _ghost_linear(h, down_idx, lut)
    x = L0_attn_hidden_states
    x = x + _layernorm(_L0_attn_ref(_layernorm(x, axis=-1), L0_attn_Wq, L0_attn_bq, L0_attn_Wk, L0_attn_bk, L0_attn_Wv, L0_attn_bv, L0_attn_Wo, L0_attn_bo, L0_attn_latent_keys), axis=-1)
    x = x + _layernorm(_L0_ffn_ref(_layernorm(x, axis=-1), L0_ffn_lut, L0_ffn_gate_idx, L0_ffn_up_idx, L0_ffn_down_idx), axis=-1)
    return x

_drawn_inputs = setup_inputs


def setup_inputs(seed=0):
    import zlib

    import numpy as np

    out = dict(_drawn_inputs(seed))
    spreads = {}
    factors = {'L0_attn_bq': 2.692}
    for name, (base, spread) in spreads.items():
        noise = np.random.default_rng([zlib.crc32(name.encode()), seed]).standard_normal(out[name].shape)
        drawn = base * np.exp(spread * noise) if base else spread * noise
        out[name] = jnp.asarray(drawn.astype(out[name].dtype))
    for name, factor in factors.items():
        out[name] = (out[name] * factor).astype(out[name].dtype)
    return out
```

```python
from contextlib import ExitStack

import concourse.bass as bass
from concourse import mybir

F32 = mybir.dt.float32
F32R = mybir.dt.float32r
I32 = mybir.dt.int32
ALU = mybir.AluOpType
ACT = mybir.ActivationFunctionType
AX_X = mybir.AxisListType.X

P = 128
T = 2048
D = 256
H = 16
HD = D // H
L = 64
K_TOP = 4
INTER = 688
LUT = 16
EPS = 1e-5

KC = D // P
NT = 2
G = T // (NT * P)
GT = NT * P
HC = H // KC
J = H * L // P
LROW = L + K_TOP
FC = INTER // P
TAIL = INTER - FC * P
TU = 64
NC = FC + 1
GUW = FC * 2 * P + P
WALL = KC * GUW + NC * D
SENTINEL = 3.0e38
MARK = -3.0e38
PIECES = [(i * GUW // 4, GUW // 4) for i in range(4 * KC)] + [(KC * GUW + i * NC * D // 4, NC * D // 4) for i in range(4)]
PW = max(w for _, w in PIECES)


def build(nc, x_d, wq_d, bq_d, wv_d, bv_d, wo_d, bo_d, lat_d, latT_d, lut_d, gi_d, ui_d, di_d, out_d):
    ctx = ExitStack()
    with ctx:
        def sb(name, shape, dt=F32):
            return ctx.enter_context(nc.sbuf_tensor(name, shape, dt))

        def sem(name):
            return ctx.enter_context(nc.semaphore(name))

        x = sb("x", [P, G * NT, D])
        ident = sb("ident", [P, P])
        half = sb("half", [P, NT])
        eps = sb("eps", [P, NT])
        minus = sb("minus", [P, NT])
        spare = sb("spare", [P, 1])
        ones = sb("ones", [1, P], F32R)
        pT = sb("pT", [P, J, GT])
        w32 = pT[:, 0:3 * KC, :].rearrange("p (i c) n -> p i c n", c=KC)
        whi = sb("whi", [P, 3, KC, D], F32R)
        wlo = sb("wlo", [P, 3, KC, D], F32R)
        bqv = sb("bqv", [P, 2, KC])
        bo32 = sb("bo32", [1, D])
        bohi = sb("bohi", [1, D], F32R)
        bolo = sb("bolo", [1, D], F32R)
        late = sb("late", [P, 2 * NT, D])
        dn, y = late[:, 0:NT, :], late[:, NT:2 * NT, :]
        lb32 = late[:, :, :].rearrange("p (c t) d -> p c (t d)", c=KC)
        lbhi = sb("lbhi", [P, KC, HC * L], F32R)
        lblo = sb("lblo", [P, KC, HC * L], F32R)
        lw = sb("lw", [P, J, 2 * HD])
        lut = sb("lut", [P, LUT])
        dlut = sb("dlut", [P, LUT // 2])
        idx = sb("idx", [P, WALL], I32)
        bits = sb("bits", [P, 4, PW], I32)
        cand = sb("cand", [P, LUT // 2, PW])
        fhi = sb("fhi", [P, WALL], F32R)
        flo = sb("flo", [P, WALL], F32R)

        KINDS = ("x", "a", "r", "d")
        st = {k: sb(f"st_{k}", [P, NT, 6]) for k in KINDS}
        mv = {k: sb(f"mv_{k}", [P, NT, 2]) for k in KINDS}
        ve = {k: sb(f"ve_{k}", [P, NT]) for k in KINDS}
        rstd = {k: sb(f"rstd_{k}", [P, NT]) for k in KINDS}
        mr = {k: sb(f"mr_{k}", [P, NT]) for k in KINDS}
        nb = {k: sb(f"nb_{k}", [P, NT]) for k in KINDS}

        xn = sb("xn", [P, NT, D])
        xThi = sb("xThi", [P, KC, GT], F32R)
        xTlo = sb("xTlo", [P, KC, GT], F32R)
        qhi = sb("qhi", [P, KC, GT], F32R)
        qlo = sb("qlo", [P, KC, GT], F32R)
        lg = [sb(f"lg{t}", [P, H, LROW]) for t in range(NT)]
        rep = [sb(f"rep{t}", [P, H, LROW]) for t in range(NT)]
        m8 = [sb(f"m8_{t}", [P, H, 8]) for t in range(NT)]
        e4 = [sb(f"e4_{t}", [P, H, K_TOP]) for t in range(NT)]
        w4 = [sb(f"w4_{t}", [P, H, K_TOP]) for t in range(NT)]
        s4 = [sb(f"s4_{t}", [P, H]) for t in range(NT)]
        r4 = [sb(f"r4_{t}", [P, H]) for t in range(NT)]
        pr = [sb(f"pr{t}", [P, H, L]) for t in range(NT)]
        mk = [sb(f"mk{t}", [P, H, L]) for t in range(NT)]
        ahi = sb("ahi", [P, KC, GT], F32R)
        alo = sb("alo", [P, KC, GT], F32R)
        an = sb("an", [P, NT, D])
        x2 = sb("x2", [P, NT, D])
        rn = sb("rn", [P, NT, D])
        rThi = sb("rThi", [P, KC, GT], F32R)
        rTlo = sb("rTlo", [P, KC, GT], F32R)
        th = sb("th", [P, 2, GT])
        ga = sb("ga", [P, 2, GT])
        h32 = sb("h32", [P, 2, GT])
        hhi = sb("hhi", [P, NC, GT], F32R)
        hlo = sb("hlo", [P, NC, GT], F32R)

        LP = [ctx.enter_context(nc.psum_tensor(f"LP{t}", [P, H * L], F32)) for t in range(NT)]
        GU = [ctx.enter_context(nc.psum_tensor(f"GU{i}", [P, 2, GT], F32)) for i in range(2)]
        X = ctx.enter_context(nc.psum_tensor("X", [P, KC, GT], F32))
        Y = ctx.enter_context(nc.psum_tensor("Y", [P, NT, D], F32))

        s_x0 = sem("x_first_loaded")
        s_xr = sem("x_rest_loaded")
        s_w = sem("attn_weights_loaded")
        s_lb = sem("latent_blocks_loaded")
        s_i = sem("indices_loaded")
        s_pad = sem("pads_cleared")
        s_cst = sem("constants_made")
        s_whi = sem("weights_hi_made")
        s_wlo = sem("weights_lo_made")
        s_dl = sem("lut_steps_made")
        s_bit = sem("index_bits_made")
        s_cand = sem("lut_candidates_made")
        s_sel = sem("lut_selected")
        s_sel_step = sem("lut_level_selected")
        s_fhi = sem("ffn_weights_hi_made")
        s_flo = sem("ffn_weights_lo_made")
        s_st = {k: sem(f"stats_{k}") for k in KINDS}
        s_mv = {k: sem(f"moments_{k}") for k in KINDS}
        s_ve = {k: sem(f"var_eps_{k}") for k in KINDS}
        s_rs = {k: sem(f"rstd_{k}_made") for k in KINDS}
        s_mr = {k: sem(f"mean_rstd_{k}") for k in KINDS}
        s_nb = {k: sem(f"ln_bias_{k}") for k in KINDS}
        s_xn = sem("xn_made")
        s_xT = sem("xT_in_psum")
        s_xThi = sem("xT_hi")
        s_xTlo = sem("xT_lo")
        s_q = sem("q_in_psum")
        s_qhi = sem("q_hi")
        s_qlo = sem("q_lo")
        s_l = sem("logits_in_psum")
        s_lg = sem("logits_in_sbuf")
        s_top = sem("top_found")
        s_rep = sem("top_marked")
        s_e4 = sem("top_shifted")
        s_w4 = sem("top_exps")
        s_s4 = sem("top_sums")
        s_r4 = sem("top_reciprocals")
        s_sh = sem("logits_shifted")
        s_ex = sem("exps")
        s_mk = sem("masks")
        s_pr = sem("probs")
        s_pT = sem("pT_in_psum")
        s_pTs = sem("pT_in_sbuf")
        s_a = sem("attn_in_psum")
        s_ahi = sem("attn_hi")
        s_alo = sem("attn_lo")
        s_o = sem("attn_out_in_psum")
        s_an = sem("attn_out_normed")
        s_x2 = sem("residual_made")
        s_rn = sem("residual_normed")
        s_rT = sem("rT_in_psum")
        s_rThi = sem("rT_hi")
        s_rTlo = sem("rT_lo")
        s_gu = sem("gate_up_in_psum")
        s_th = sem("tanh_made")
        s_ga = sem("gate_made")
        s_h = sem("h_made")
        s_hhi = sem("h_hi")
        s_hlo = sem("h_lo")
        s_dn = sem("down_in_psum")
        s_dnn = sem("down_normed")
        s_y = sem("out_made")
        s_out = sem("out_stored")

        N_LB = HC + 2

        def after(eng, s, value):
            if not isinstance(value, int) or value > 0:
                eng.wait_ge(s, value)

        block = ctx.enter_context(nc.Block())

        @block.sync
        def _(sp):
            xg = x_d.rearrange("(g t p) d -> g p t d", p=P, t=NT)
            sp.dma_start(x[:, 0:NT, :], xg[0]).then_inc(s_x0, 16)
            sp.dma_start(w32[:, 0, :, :], wq_d.rearrange("(c p) n -> p c n", p=P)).then_inc(s_w, 16)
            sp.dma_start(bqv[:, 0, :], bq_d).then_inc(s_w, 16)
            sp.dma_start(bqv[:, 1, :], bv_d).then_inc(s_w, 16)
            sp.wait_ge(s_pad, 1)
            for h in range(HC):
                sp.dma_start(lb32[h * HD:(h + 1) * HD, :, h * L:(h + 1) * L],
                             latT_d.rearrange("(c h d) l -> h d c l", c=KC, h=HC)[h]).then_inc(s_lb, 16)
            for e in range(2):
                sp.dma_start(lw[e * L:(e + 1) * L, :, e * HD:(e + 1) * HD],
                             lat_d.rearrange("l (j e d) -> e l j d", e=2, d=HD)[e]).then_inc(s_lb, 16)
            sp.dma_start(w32[:, 1, :, :], wv_d.rearrange("(c p) n -> p c n", p=P)).then_inc(s_w, 16)
            sp.dma_start(w32[:, 2, :, :], wo_d.rearrange("(c p) n -> p c n", p=P)).then_inc(s_w, 16)
            sp.dma_start(bo32[:, :], bo_d.rearrange("(a n) -> a n", a=1)).then_inc(s_w, 16)
            for g in range(1, G):
                sp.dma_start(x[:, g * NT:(g + 1) * NT, :], xg[g]).then_inc(s_xr, 16)

            def store(g):
                sp.wait_ge(s_y, g + 1)
                sp.dma_start(out_d[bass.ds(g * GT, GT), :].rearrange("(t p) d -> p t d", p=P), y[:, :, :])\
                  .then_inc(s_out, 16)

            with sp.Fori(0, G) as g:
                store(g)
            sp.wait_ge(s_out, 16 * (G + 1))

        @block.tensor
        def _(pe):
            def split3(out, lhs, rhs, first, last, skip=False):
                (lh, ll), (rh, rl) = lhs, rhs
                pe.matmul(out, lh, rh, start=first, stop=False, skip_group_check=skip)
                pe.matmul(out, lh, rl, start=False, stop=False, skip_group_check=skip)
                return pe.matmul(out, ll, rh, start=False, stop=last, skip_group_check=skip)

            def front(g):
                pe.wait_ge(s_xn, g + 1)
                for t in range(NT):
                    for c in range(KC):
                        last = pe.transpose(X[:, c, t * P:(t + 1) * P], xn[:, t, c * P:(c + 1) * P], ident[:, :])
                last.then_inc(s_xT, 1)
                pe.wait_ge(s_xThi, g + 1)
                pe.wait_ge(s_xTlo, g + 1)
                for m in range(KC):
                    for c in range(KC):
                        last = split3(GU[0][:, m, :],
                                      [w[:, 0, c, m * P:(m + 1) * P] for w in (whi, wlo)],
                                      [w[:, c, :] for w in (xThi, xTlo)], c == 0, c == KC - 1)
                last.then_inc(s_q, 1)
                pe.wait_ge(s_qhi, g + 1)
                pe.wait_ge(s_qlo, g + 1)
                for t in range(NT):
                    for c in range(KC):
                        last = split3(LP[t][:, c * HC * L:(c + 1) * HC * L],
                                      [w[:, c, t * P:(t + 1) * P] for w in (qhi, qlo)],
                                      [w[:, c, :] for w in (lbhi, lblo)], True, True)
                    last.then_inc(s_l, 1)

            def attend(g):
                for m in range(KC):
                    for c in range(KC):
                        split3(X[:, m, :], [w[:, 1, c, m * P:(m + 1) * P] for w in (whi, wlo)],
                               [w[:, c, :] for w in (xThi, xTlo)], m == 0 and c == 0, False, skip=True)
                for t in range(NT):
                    pe.wait_ge(s_pr, NT * g + t + 1)
                    for j in range(J):
                        last = pe.transpose(LP[t][:, j * P:(j + 1) * P],
                                            pr[t][:, 2 * j:2 * j + 2, :].rearrange("p h l -> p (h l)"), ident[:, :])
                    last.then_inc(s_pT, 1)
                pe.wait_ge(s_pTs, NT * g + NT)
                for j in range(J):
                    r, m = 32 * (j % 4), j // 4
                    last = pe.matmul(X[r:r + 2 * HD, m, :], lw[:, j, :], pT[:, j, :], start=False,
                                     stop=True, skip_group_check=True)
                last.then_inc(s_a, 1)
                pe.wait_ge(s_ahi, g + 1)
                pe.wait_ge(s_alo, g + 1)
                after(pe, s_dnn, g)
                for t in range(NT):
                    pe.matmul(Y[:, t, :], ones[:, :], bohi[:, :], start=True, stop=False)
                    pe.matmul(Y[:, t, :], ones[:, :], bolo[:, :], start=False, stop=False)
                    for c in range(KC):
                        last = split3(Y[:, t, :], [w[:, c, t * P:(t + 1) * P] for w in (ahi, alo)],
                                      [w[:, 2, c, :] for w in (whi, wlo)], False, c == KC - 1)
                last.then_inc(s_o, 1)

            def turn_residual(g):
                pe.wait_ge(s_rn, g + 1)
                for t in range(NT):
                    for c in range(KC):
                        last = pe.transpose(X[:, c, t * P:(t + 1) * P], rn[:, t, c * P:(c + 1) * P], ident[:, :])
                last.then_inc(s_rT, 1)

            def gate_up(g):
                pe.wait_ge(s_rThi, g + 1)
                pe.wait_ge(s_rTlo, g + 1)
                for f in range(NC):
                    if f >= 2:
                        pe.wait_ge(s_h, NC * g + f - 1)
                    if f < FC:
                        for u in range(2):
                            for c in range(KC):
                                at = c * GUW + (2 * f + u) * P
                                last = split3(GU[f % 2][:, u, :], [w[:, at:at + P] for w in (fhi, flo)],
                                              [w[:, c, :] for w in (rThi, rTlo)], c == 0, c == KC - 1)
                    else:
                        for c in range(KC):
                            at = c * GUW + 2 * FC * P
                            last = split3(GU[f % 2][:, 0, :], [w[:, at:at + P] for w in (fhi, flo)],
                                          [w[:, c, :] for w in (rThi, rTlo)], c == 0, c == KC - 1)
                    last.then_inc(s_gu, 1)

            def down(g):
                for f in range(NC):
                    rows = P if f < FC else TAIL
                    pe.wait_ge(s_hhi, NC * g + f + 1)
                    pe.wait_ge(s_hlo, NC * g + f + 1)
                    at = KC * GUW + f * D
                    for t in range(NT):
                        last = split3(Y[:, t, :], [w[0:rows, f, t * P:(t + 1) * P] for w in (hhi, hlo)],
                                      [w[0:rows, at:at + D] for w in (fhi, flo)], f == 0 and t == 0, f == NC - 1,
                                      skip=True)
                last.then_inc(s_dn, 1)

            def body(g):
                front(g + 1)
                turn_residual(g)
                gate_up(g)
                down(g)
                attend(g + 1)

            pe.wait_ge(s_cst, 2)
            pe.wait_ge(s_whi, 5)
            pe.wait_ge(s_wlo, 5)
            pe.wait_ge(s_lb, 16 * N_LB)
            front(0)
            attend(0)
            pe.wait_ge(s_fhi, len(PIECES))
            pe.wait_ge(s_flo, len(PIECES))
            with pe.Fori(0, G - 2) as g:
                body(g)
            body(G - 2)
            turn_residual(G - 1)
            gate_up(G - 1)
            down(G - 1)

        @block.scalar
        def _(act):
            act.dma_start(lut[:, :], lut_d.rearrange("(a n) -> a n", a=1).broadcast_to([P, LUT])).then_inc(s_i, 16)
            act.wait_ge(s_pad, 3)
            for c in range(KC):
                at = c * GUW
                pair = idx[:, at:at + 2 * FC * P].rearrange("p (f u n) -> p f u n", u=2, n=P)
                for u, src in ((0, gi_d), (1, ui_d)):
                    rows = src[c * P:(c + 1) * P, :]
                    act.dma_start(pair[:, :, u, :], rows[:, 0:FC * P].rearrange("p (f n) -> p f n", n=P))\
                       .then_inc(s_i, 16)
                    act.dma_start(idx[:, at + 2 * FC * P + u * TU:at + 2 * FC * P + u * TU + TAIL],
                                  rows[:, FC * P:INTER]).then_inc(s_i, 16)
            at = KC * GUW
            act.dma_start(idx[:, at:at + FC * D].rearrange("p (f n) -> p f n", n=D),
                          di_d[0:FC * P, :].rearrange("(f p) n -> p f n", p=P)).then_inc(s_i, 16)
            act.dma_start(idx[0:TAIL, at + FC * D:at + NC * D], di_d[FC * P:INTER, :]).then_inc(s_i, 16)

            def apply(k, dst, src, g, done, tiles):
                act.wait_ge(s_nb[k], g + 1)
                for t in range(NT):
                    last = act.activation(dst[:, t, :], src(t), ACT.Identity, bias=nb[k][:, t:t + 1],
                                          scale=rstd[k][:, t:t + 1])
                last.then_inc(done, 1)

            def norm_x(g):
                after(act, s_xT, g)
                apply("x", xn, lambda t: x[:, NT * g + t, :] if isinstance(g, int)
                      else x[:, bass.ds(NT * g + t, 1), :].rearrange("p a d -> p (a d)"), g, s_xn, None)

            def xT(g):
                act.wait_ge(s_xT, g + 1)
                act.activation(xThi[:, :, :], X[:, :, :], ACT.Copy).then_inc(s_xThi, 1)

            def q(g):
                act.wait_ge(s_q, g + 1)
                for m in range(KC):
                    last = act.activation(qhi[:, m, :], GU[0][:, m, :], ACT.Identity, bias=bqv[:, 0, m:m + 1])
                last.then_inc(s_qhi, 1)

            def logits(g, t):
                act.wait_ge(s_l, NT * g + t + 1)
                after(act, s_mk, NT * (g - 1) + t + 1)
                after(act, s_sh, NT * (g - 1) + t + 1)
                act.activation(lg[t][:, :, 0:L], LP[t][:, :].rearrange("p (h l) -> p h l", l=L), ACT.Copy)\
                   .then_inc(s_lg, 1)

            def exps(g, t):
                act.wait_ge(s_sh, NT * g + t + 1)
                act.activation(pr[t][:, :, :], pr[t][:, :, :], ACT.Exp, scale=HD ** -0.5).then_inc(s_ex, 1)

            def top_exps(g, t):
                act.wait_ge(s_e4, NT * g + t + 1)
                act.activation(w4[t][:, :, :], e4[t][:, :, :], ACT.Exp, scale=HD ** -0.5).then_inc(s_w4, 1)

            def probs_turned(g, t):
                act.wait_ge(s_pT, NT * g + t + 1)
                act.activation(pT[:, :, t * P:(t + 1) * P], LP[t][:, :].rearrange("p (j n) -> p j n", n=P), ACT.Copy)\
                   .then_inc(s_pTs, 1)

            def attn(g):
                act.wait_ge(s_a, g + 1)
                for m in range(KC):
                    last = act.activation(ahi[:, m, :], X[:, m, :], ACT.Identity, bias=bqv[:, 1, m:m + 1])
                last.then_inc(s_ahi, 1)

            def norm_attn(g):
                apply("a", an, lambda t: Y[:, t, :], g, s_an, None)

            def norm_residual(g):
                apply("r", rn, lambda t: x2[:, t, :], g, s_rn, None)

            def rT(g):
                act.wait_ge(s_rT, g + 1)
                act.activation(rThi[:, :, :], X[:, :, :], ACT.Copy).then_inc(s_rThi, 1)

            def tanh(g, f):
                rows = P if f < FC else TAIL
                act.wait_ge(s_gu, NC * g + f + 1)
                act.activation(th[0:rows, f % 2, :], GU[f % 2][0:rows, 0, :], ACT.Tanh, scale=0.5).then_inc(s_th, 1)

            def h_hi(g, f):
                rows = P if f < FC else TAIL
                act.wait_ge(s_h, NC * g + f + 1)
                act.activation(hhi[0:rows, f, :], h32[0:rows, f % 2, :], ACT.Copy).then_inc(s_hhi, 1)

            def norm_down(g):
                apply("d", dn, lambda t: Y[:, t, :], g, s_dnn, None)

            def front_part(g):
                xT(g)
                q(g)

            act.wait_ge(s_w, 16 * 6)
            act.wait_ge(s_lb, 16 * N_LB)
            act.activation(lbhi[:, :, :], lb32[:, :, :], ACT.Copy).then_inc(s_whi, 1)
            for i in range(3):
                act.activation(whi[:, i, :, :], w32[:, i, :, :], ACT.Copy).then_inc(s_whi, 1)
            act.activation(bohi[:, :], bo32[:, :], ACT.Copy).then_inc(s_whi, 1)
            norm_x(0)
            xT(0)
            q(0)
            logits(0, 0)
            logits(0, 1)
            exps(0, 0)
            top_exps(0, 0)
            exps(0, 1)
            top_exps(0, 1)
            norm_x(1)
            probs_turned(0, 0)
            probs_turned(0, 1)
            attn(0)
            for i, (a, w) in enumerate(PIECES):
                act.wait_ge(s_bit, i + 1)
                for j in range(LUT // 2):
                    last = act.activation(cand[:, j, 0:w], bits[:, 0, 0:w], ACT.Identity,
                                          bias=lut[:, 2 * j:2 * j + 1], scale=dlut[:, j:j + 1])
                last.then_inc(s_cand, 1)
                act.wait_ge(s_sel, i + 1)
                act.activation(fhi[:, a:a + w], cand[:, 0, 0:w], ACT.Copy, scale=1.0 if a < KC * GUW else 0.5)\
                   .then_inc(s_fhi, 1)

            def body(g, front=True, ahead=True):
                if front:
                    xT(g + 1)
                norm_attn(g)
                if front:
                    q(g + 1)
                    logits(g + 1, 0)
                norm_residual(g)
                if front:
                    logits(g + 1, 1)
                rT(g)
                if front:
                    top_exps(g + 1, 0)
                    exps(g + 1, 0)
                tanh(g, 0)
                for f in range(1, NC):
                    tanh(g, f)
                    h_hi(g, f - 1)
                    if front and f == 3:
                        top_exps(g + 1, 1)
                        exps(g + 1, 1)
                h_hi(g, NC - 1)
                if ahead:
                    norm_x(g + 2)
                if front:
                    probs_turned(g + 1, 0)
                    probs_turned(g + 1, 1)
                norm_down(g)
                if front:
                    attn(g + 1)

            with act.Fori(0, G - 2) as g:
                body(g)
            body(G - 2, ahead=False)
            body(G - 1, front=False, ahead=False)

        @block.vector
        def _(dve):
            def held():
                dve.memset(spare[:, :], 0.0)

            def stats(k, src, g):
                for t in range(NT):
                    last = dve.bn_stats(st[k][:, t, :], src(t))
                last.then_inc(s_st[k], 1)
                dve.wait_ge(s_st[k], g + 1)
                held()
                for t in range(NT):
                    last = dve.bn_aggr(mv[k][:, t, :], st[k][:, t, :])
                last.then_inc(s_mv[k], 1)

            def stats_x(g):
                stats("x", lambda t: x[:, NT * g + t, :] if isinstance(g, int)
                      else x[:, bass.ds(NT * g + t, 1), :].rearrange("p a d -> p (a d)"), g)

            def stats_attn(g):
                dve.wait_ge(s_o, g + 1)
                stats("a", lambda t: Y[:, t, :], g)

            def stats_residual(g):
                dve.wait_ge(s_x2, g + 1)
                stats("r", lambda t: x2[:, t, :], g)

            def stats_down(g):
                dve.wait_ge(s_dn, g + 1)
                stats("d", lambda t: Y[:, t, :], g)

            def low(dst, src, hi, done):
                return dve.tensor_tensor(dst, src, hi.bitcast(F32), ALU.subtract).then_inc(done, 1)

            def xT(g):
                dve.wait_ge(s_xThi, g + 1)
                low(xTlo[:, :, :], X[:, :, :], xThi[:, :, :], s_xTlo)

            def biased_low(dst, src, bias, hi):
                return dve.scalar_tensor_tensor(dst, src, bias, hi.bitcast(F32), ALU.add, ALU.subtract)

            def q(g):
                dve.wait_ge(s_qhi, g + 1)
                for m in range(KC):
                    last = biased_low(qlo[:, m, :], GU[0][:, m, :], bqv[:, 0, m:m + 1], qhi[:, m, :])
                last.then_inc(s_qlo, 1)

            def attn(g):
                dve.wait_ge(s_ahi, g + 1)
                for m in range(KC):
                    last = biased_low(alo[:, m, :], X[:, m, :], bqv[:, 1, m:m + 1], ahi[:, m, :])
                last.then_inc(s_alo, 1)

            def rT(g):
                dve.wait_ge(s_rThi, g + 1)
                low(rTlo[:, :, :], X[:, :, :], rThi[:, :, :], s_rTlo)

            def top(g, t, a=0, b=H):
                if a == 0:
                    dve.wait_ge(s_lg, NT * g + t + 1)
                    after(dve, s_sh, NT * (g - 1) + t + 1)
                    held()
                for h in range(a, b):
                    last = dve.max(m8[t][:, h, :], lg[t][:, h, :])
                if b == H:
                    last.then_inc(s_top, 1)

            def mark(g, t, a=0, b=H):
                for h in range(a, b):
                    last = dve.match_replace(rep[t][:, h, :], m8[t][:, h, :], lg[t][:, h, :], MARK)
                if b == H:
                    last.then_inc(s_rep, 1)

            def shift_top(g, t):
                dve.wait_ge(s_top, NT * g + t + 1)
                dve.tensor_tensor(e4[t][:, :, :], m8[t][:, :, K_TOP:2 * K_TOP],
                                  m8[t][:, :, K_TOP:K_TOP + 1].broadcast_to([P, H, K_TOP]), ALU.subtract)\
                   .then_inc(s_e4, 1)

            def masks(g, t):
                dve.wait_ge(s_w4, NT * g + t + 1)
                dve.tensor_reduce(s4[t][:, :], w4[t][:, :, :], AX_X, ALU.add).then_inc(s_s4, 1)
                dve.wait_ge(s_s4, NT * g + t + 1)
                dve.reciprocal(r4[t][:, :], s4[t][:, :]).then_inc(s_r4, 1)
                dve.wait_ge(s_r4, NT * g + t + 1)
                dve.wait_ge(s_rep, NT * g + t + 1)
                after(dve, s_pr, NT * (g - 1) + t + 1)
                dve.scalar_tensor_tensor(mk[t][:, :, :], rep[t][:, :, 0:L], MARK,
                                         r4[t][:, :].rearrange("p (h a) -> p h a", a=1).broadcast_to([P, H, L]),
                                         ALU.is_equal, ALU.mult).then_inc(s_mk, 1)

            def gate(g, f):
                rows, at, u = (P, 0, 1) if f < FC else (TAIL, TU, 0)
                dve.wait_ge(s_th, NC * g + f + 1)
                dve.scalar_tensor_tensor(ga[0:rows, f % 2, :], th[0:rows, f % 2, :], 1.0, GU[f % 2][0:rows, 0, :],
                                         ALU.add, ALU.mult).then_inc(s_ga, 1)
                dve.wait_ge(s_ga, NC * g + f + 1)
                if f >= 2:
                    dve.wait_ge(s_hhi, NC * g + f - 1)
                    dve.wait_ge(s_hlo, NC * g + f - 1)
                dve.tensor_tensor(h32[0:rows, f % 2, :], ga[0:rows, f % 2, :],
                                  GU[f % 2][at:at + rows, u, :], ALU.mult).then_inc(s_h, 1)

            dve.wait_ge(s_x0, 16)
            stats_x(0)
            dve.wait_ge(s_whi, 1)
            low(lblo[:, :, :], lb32[:, :, :], lbhi[:, :, :], s_wlo)
            for i in range(3):
                dve.wait_ge(s_whi, i + 2)
                low(wlo[:, i, :, :], w32[:, i, :, :], whi[:, i, :, :], s_wlo)
            dve.wait_ge(s_whi, 5)
            low(bolo[:, :], bo32[:, :], bohi[:, :], s_wlo)
            xT(0)
            q(0)
            top(0, 0)
            shift_top(0, 0)
            mark(0, 0)
            masks(0, 0)
            top(0, 1)
            shift_top(0, 1)
            mark(0, 1)
            masks(0, 1)
            dve.wait_ge(s_xr, 16 * (G - 1))
            stats_x(1)
            attn(0)
            dve.wait_ge(s_i, 16 * (3 + 4 * KC))
            pairs = lut[:, :].rearrange("p (j e) -> p j e", e=2)
            dve.tensor_tensor(dlut[:, :], pairs[:, :, 1], pairs[:, :, 0], ALU.subtract).then_inc(s_dl, 1)
            n_sel = 0
            for i, (a, w) in enumerate(PIECES):
                if i:
                    dve.wait_ge(s_fhi, i)
                dve.wait_ge(s_sel, i) if i else None
                for b in range(4):
                    last = dve.tensor_scalar(bits[:, b, 0:w], idx[:, a:a + w], 1 << b, None, ALU.bitwise_and)
                if i == 0:
                    dve.wait_ge(s_dl, 1)
                last.then_inc(s_bit, 1)
                dve.wait_ge(s_bit, i + 1)
                dve.wait_ge(s_cand, i + 1)
                for b in range(1, 4):
                    step = 1 << (b - 1)
                    for j in range(0, LUT // 2, 2 * step):
                        last = dve.copy_predicated(cand[:, j, 0:w], bits[:, b, 0:w], cand[:, j + step, 0:w])
                        n_sel += 1
                    if b < 3:
                        last.then_inc(s_sel_step, 1)
                        dve.wait_ge(s_sel_step, 2 * i + b)
                last.then_inc(s_sel, 1)
                dve.wait_ge(s_sel, i + 1)
                dve.wait_ge(s_fhi, i + 1)
                dve.scalar_tensor_tensor(flo[:, a:a + w], cand[:, 0, 0:w], 1.0 if a < KC * GUW else 0.5,
                                         fhi[:, a:a + w].bitcast(F32), ALU.mult, ALU.subtract).then_inc(s_flo, 1)
                dve.wait_ge(s_flo, i + 1)

            def body(g, front=True, ahead=True):
                if front:
                    xT(g + 1)
                stats_attn(g)
                if front:
                    q(g + 1)
                    top(g + 1, 0)
                    shift_top(g + 1, 0)
                stats_residual(g)
                if front:
                    mark(g + 1, 0)
                rT(g)
                if front:
                    masks(g + 1, 0)
                    top(g + 1, 1, 0, HC)
                gate(g, 0)
                if front:
                    top(g + 1, 1, HC, H)
                    shift_top(g + 1, 1)
                gate(g, 1)
                if front:
                    mark(g + 1, 1, 0, HC)
                gate(g, 2)
                if front:
                    mark(g + 1, 1, HC, H)
                gate(g, 3)
                if front:
                    masks(g + 1, 1)
                gate(g, 4)
                gate(g, 5)
                if ahead:
                    stats_x(g + 2)
                stats_down(g)
                if front:
                    attn(g + 1)

            with dve.Fori(0, G - 2) as g:
                body(g)
            body(G - 2, ahead=False)
            body(G - 1, front=False, ahead=False)

        @block.gpsimd
        def _(pool):
            pool.memset(lb32[:, :, :], 0.0)
            pool.memset(lw[:, :, :], 0.0).then_inc(s_pad, 1)
            for c in range(KC):
                pool.memset(idx[:, c * GUW + 2 * FC * P:(c + 1) * GUW], 0)
            pool.memset(idx[:, KC * GUW + FC * D:WALL], 0).then_inc(s_pad, 2)
            pool.memset(half[:, :], -0.5)
            pool.memset(eps[:, :], EPS)
            pool.memset(minus[:, :], -1.0).then_inc(s_out, 16)
            pool.memset(ones[:, :].bitcast(F32), 1.0)
            for t in range(NT):
                pool.memset(lg[t][:, :, L:LROW], SENTINEL)
            pool.memset(ident[:, :], 0.0).then_inc(s_cst, 1)
            pool.wait_ge(s_cst, 1)
            pool.affine_select(out=ident[:, :], in_=ident[:, :], compare_op=ALU.not_equal, fill=1.0,
                               base=0, pattern=[[-1, P]], channel_multiplier=1).then_inc(s_cst, 1)
            pool.wait_ge(s_cst, 2)

            def rstds(k, g):
                pool.wait_ge(s_mv[k], g + 1)
                pool.tensor_tensor(ve[k][:, :], mv[k][:, :, 1], eps[:, :], ALU.add).then_inc(s_ve[k], 1)
                pool.wait_ge(s_ve[k], g + 1)
                pool.tensor_tensor(rstd[k][:, :], ve[k][:, :], half[:, :], ALU.pow).then_inc(s_rs[k], 1)
                pool.wait_ge(s_rs[k], g + 1)
                pool.tensor_tensor(mr[k][:, :], mv[k][:, :, 0], rstd[k][:, :], ALU.mult).then_inc(s_mr[k], 1)
                pool.wait_ge(s_mr[k], g + 1)
                pool.tensor_tensor(nb[k][:, :], mr[k][:, :], minus[:, :], ALU.mult).then_inc(s_nb[k], 1)

            def residual(g):
                pool.wait_ge(s_an, g + 1)
                src = x[:, NT * g:NT * g + NT, :] if isinstance(g, int) else x[:, bass.ds(NT * g, NT), :]
                pool.tensor_tensor(x2[:, :, :], an[:, :, :], src, ALU.add).then_inc(s_x2, 1)

            def shift(g, t):
                pool.wait_ge(s_top, NT * g + t + 1)
                after(pool, s_pT, NT * (g - 1) + t + 1)
                pool.tensor_tensor(pr[t][:, :, :], lg[t][:, :, 0:L],
                                   m8[t][:, :, K_TOP:K_TOP + 1].broadcast_to([P, H, L]), ALU.subtract)\
                    .then_inc(s_sh, 1)

            def probs(g, t):
                pool.wait_ge(s_ex, NT * g + t + 1)
                pool.wait_ge(s_mk, NT * g + t + 1)
                pool.tensor_tensor(pr[t][:, :, :], pr[t][:, :, :], mk[t][:, :, :], ALU.mult).then_inc(s_pr, 1)

            def h_lo(g, f):
                rows = P if f < FC else TAIL
                pool.wait_ge(s_hhi, NC * g + f + 1)
                pool.tensor_tensor(hlo[0:rows, f, :], h32[0:rows, f % 2, :], hhi[0:rows, f, :].bitcast(F32),
                                   ALU.subtract).then_inc(s_hlo, 1)

            def output(g):
                pool.wait_ge(s_dnn, g + 1)
                pool.wait_ge(s_out, 16 * (g + 1))
                pool.tensor_tensor(y[:, :, :], dn[:, :, :], x2[:, :, :], ALU.add).then_inc(s_y, 1)

            rstds("x", 0)
            shift(0, 0)
            probs(0, 0)
            shift(0, 1)
            probs(0, 1)
            rstds("x", 1)

            def body(g, front=True, ahead=True):
                rstds("a", g)
                residual(g)
                rstds("r", g)
                if front:
                    shift(g + 1, 0)
                    probs(g + 1, 0)
                h_lo(g, 0)
                h_lo(g, 1)
                if front:
                    shift(g + 1, 1)
                h_lo(g, 2)
                h_lo(g, 3)
                if front:
                    probs(g + 1, 1)
                h_lo(g, 4)
                h_lo(g, 5)
                if ahead:
                    rstds("x", g + 2)
                rstds("d", g)
                output(g)

            with pool.Fori(0, G - 2) as g:
                body(g)
            body(G - 2, ahead=False)
            body(G - 1, front=False, ahead=False)


def kernel(**inputs):
    import numpy as np
    import concourse.bacc as bacc
    from concourse.bass_utils import run_bass_kernel_spmd

    def a(name):
        return np.asarray(inputs[name])

    lay = np.ascontiguousarray
    arrays = {
        "x_in": lay(a("L0_attn_hidden_states")[0]),
        "wq_in": lay(a("L0_attn_Wq").T), "bq_in": lay(a("L0_attn_bq").reshape(KC, P).T),
        "wv_in": lay(a("L0_attn_Wv").T), "bv_in": lay(a("L0_attn_bv").reshape(KC, P).T),
        "wo_in": lay(a("L0_attn_Wo").T), "bo_in": lay(a("L0_attn_bo")),
        "lat_in": lay(a("L0_attn_latent_keys")), "latT_in": lay(a("L0_attn_latent_keys").T),
        "lut_in": lay(a("L0_ffn_lut")),
        "gate_in": lay(a("L0_ffn_gate_idx").T), "up_in": lay(a("L0_ffn_up_idx").T),
        "down_in": lay(a("L0_ffn_down_idx").T),
    }
    nc = bacc.Bacc("TRN2", target_bir_lowering=False, num_devices=1)
    args = [nc.dram_tensor(n, v.shape, mybir.dt.from_np(v.dtype), kind="ExternalInput").ap() for n, v in arrays.items()]
    out = nc.dram_tensor("out", (T, D), F32, kind="ExternalOutput").ap()
    build(nc, *args, out)
    r = run_bass_kernel_spmd(nc, [arrays], core_ids=[0])
    return r.results[0]["out"].reshape(1, T, D)
```

```python
from contextlib import ExitStack

import concourse.bass as bass
from concourse import mybir

F32 = mybir.dt.float32
F32R = mybir.dt.float32r
BF16 = mybir.dt.bfloat16
I32 = mybir.dt.int32
ALU = mybir.AluOpType
ACT = mybir.ActivationFunctionType
AX_X = mybir.AxisListType.X

P = 128
T = 2048
D = 256
H = 16
HD = D // H
L = 64
K_TOP = 4
INTER = 688
LUT = 16
EPS = 1e-5

KC = D // P
NT = 2
G = T // (NT * P)
GT = NT * P
HC = H // KC
J = H * L // P
LROW = L + K_TOP
FC = INTER // P
TAIL = INTER - FC * P
TU = 64
NC = FC + 1
GUW = FC * 2 * P + P
WALL = KC * GUW + NC * D
SENTINEL = 3.0e38
MARK = -3.0e38
PW = 256
PIECES = WALL // PW
RB = 32
NB = P // RB
STEPS = LUT // NB
PARTS = 3
IDX_ENDS = [(c + 1) * GUW for c in range(KC)] + [WALL]
PHASES = [(0, 6), (6, 12), (12, PIECES)]


def build(nc, x_d, wq_d, bq_d, wv_d, bv_d, wo_d, bo_d, lat_d, latT_d, lut_d, gi_d, ui_d, di_d, out_d):
    ctx = ExitStack()
    with ctx:
        def sb(name, shape, dt=F32):
            return ctx.enter_context(nc.sbuf_tensor(name, shape, dt))

        def sem(name):
            return ctx.enter_context(nc.semaphore(name))

        x = sb("x", [P, G * NT, D])
        ident = sb("ident", [P, P])
        half = sb("half", [P, NT])
        spare = sb("spare", [P, 8])
        ones = sb("ones", [1, P], F32R)
        pT = sb("pT", [P, J, GT])
        w32 = pT[:, 0:3 * KC, :].rearrange("p (i c) n -> p i c n", c=KC)
        whi = sb("whi", [P, 3, KC, D], F32R)
        wlo = sb("wlo", [P, 3, KC, D], F32R)
        bqv = sb("bqv", [P, 2, KC])
        bo32 = sb("bo32", [1, D])
        bohi = sb("bohi", [1, D], F32R)
        bolo = sb("bolo", [1, D], F32R)
        late = sb("late", [P, 2 * NT, D])
        dn, y = late[:, 0:NT, :], late[:, NT:2 * NT, :]
        lb32 = late[:, :, :].rearrange("p (c t) d -> p c (t d)", c=KC)
        lbhi = sb("lbhi", [P, KC, HC * L], F32R)
        lblo = sb("lblo", [P, KC, HC * L], F32R)
        lw = sb("lw", [P, J, 2 * HD])
        lut = sb("lut", [P, LUT])
        vlut = sb("vlut", [P, STEPS])
        nv = sb("nv", [P, 1])
        rest = sb("rest", [P, 2, STEPS])
        parts = sb("parts", [P, STEPS, PARTS], BF16)
        eye = sb("eye", [P, P], BF16)
        eye32 = sb("eye32", [P, RB], BF16)
        pick = sb("pick", [P, STEPS, PARTS, RB], BF16)
        spread = sb("spread", [P, NB, NB, RB], BF16)
        idx = sb("idx", [P, WALL], I32)
        idxb = sb("idxb", [P, WALL], BF16)
        rep = sb("rep", [P, 2, NB * PW], BF16)
        hot = sb("hot", [P, STEPS, NB * PW], BF16)
        fhi = sb("fhi", [P, WALL], F32R)
        flo = sb("flo", [P, WALL], F32R)

        KINDS = ("x", "a", "r", "d")
        st = {k: sb(f"st_{k}", [P, NT, 6]) for k in KINDS}
        mv = {k: sb(f"mv_{k}", [P, NT, 2]) for k in KINDS}
        ve = {k: sb(f"ve_{k}", [P, NT]) for k in KINDS}
        nm = {k: sb(f"nm_{k}", [P, NT]) for k in KINDS}
        rstd = {k: sb(f"rstd_{k}", [P, NT]) for k in KINDS}
        nb = {k: sb(f"nb_{k}", [P, NT]) for k in KINDS}

        xn = sb("xn", [P, NT, D])
        xThi = sb("xThi", [P, KC, GT], F32R)
        xTlo = sb("xTlo", [P, KC, GT], F32R)
        qhi = sb("qhi", [P, KC, GT], F32R)
        qlo = sb("qlo", [P, KC, GT], F32R)
        lg = [sb(f"lg{t}", [P, H, LROW]) for t in range(NT)]
        marked = [sb(f"marked{t}", [P, H, LROW]) for t in range(NT)]
        m8 = [sb(f"m8_{t}", [P, H, 8]) for t in range(NT)]
        e4 = [sb(f"e4_{t}", [P, H, K_TOP]) for t in range(NT)]
        w4 = [sb(f"w4_{t}", [P, H, K_TOP]) for t in range(NT)]
        s4 = [sb(f"s4_{t}", [P, H]) for t in range(NT)]
        r4 = [sb(f"r4_{t}", [P, H]) for t in range(NT)]
        pr = [sb(f"pr{t}", [P, H, L]) for t in range(NT)]
        mk = [sb(f"mk{t}", [P, H, L]) for t in range(NT)]
        ahi = sb("ahi", [P, KC, GT], F32R)
        alo = sb("alo", [P, KC, GT], F32R)
        an = sb("an", [P, NT, D])
        rn = sb("rn", [P, NT, D])
        rThi = sb("rThi", [P, KC, GT], F32R)
        rTlo = sb("rTlo", [P, KC, GT], F32R)
        th = sb("th", [P, 2, GT])
        ga = sb("ga", [P, 2, GT])
        h32 = sb("h32", [P, 2, GT])
        hhi = sb("hhi", [P, NC, GT], F32R)
        hlo = sb("hlo", [P, NC, GT], F32R)

        LP = [ctx.enter_context(nc.psum_tensor(f"LP{t}", [P, H * L], F32)) for t in range(NT)]
        GU = [ctx.enter_context(nc.psum_tensor(f"GU{i}", [P, 2, GT], F32)) for i in range(2)]
        X = ctx.enter_context(nc.psum_tensor("X", [P, KC, GT], F32))
        Y = ctx.enter_context(nc.psum_tensor("Y", [P, NT, D], F32))

        s_x0 = sem("x_first_loaded")
        s_xr = sem("x_rest_loaded")
        s_w = sem("attn_weights_loaded")
        s_lb = sem("latent_blocks_loaded")
        s_i = [sem(f"indices_loaded_{i}") for i in range(len(IDX_ENDS))]
        s_v = sem("lut_loaded")
        s_pad = sem("pads_cleared")
        s_cst = sem("constants_made")
        s_whi = sem("weights_hi_made")
        s_wlo = sem("weights_lo_made")
        s_eye = sem("bf16_identities_made")
        s_e32 = sem("block_identity_made")
        s_nv = sem("partition_values_made")
        s_vl = sem("lut_by_partition")
        s_part = sem("lut_parts_made")
        s_pick = sem("lookup_stationaries_made")
        s_ib = sem("indices_in_bf16")
        s_rp = sem("indices_spread_in_psum")
        s_rc = sem("indices_spread")
        s_hot = sem("one_hot_made")
        s_used = sem("one_hot_used")
        s_fhi = sem("ffn_weights_hi_made")
        s_flo = sem("ffn_weights_lo_made")
        s_st = {k: sem(f"stats_{k}") for k in KINDS}
        s_mv = {k: sem(f"moments_{k}") for k in KINDS}
        s_ve = {k: sem(f"var_eps_{k}") for k in KINDS}
        s_rs = {k: sem(f"rstd_{k}_made") for k in KINDS}
        s_nb = {k: sem(f"ln_bias_{k}") for k in KINDS}
        s_xn = sem("xn_made")
        s_xT = sem("xT_in_psum")
        s_xThi = sem("xT_hi")
        s_xTlo = sem("xT_lo")
        s_q = sem("q_in_psum")
        s_qhi = sem("q_hi")
        s_qlo = sem("q_lo")
        s_l = sem("logits_in_psum")
        s_lg = sem("logits_in_sbuf")
        s_top = sem("top_found")
        s_marked = sem("top_marked")
        s_e4 = sem("top_shifted")
        s_w4 = sem("top_exps")
        s_s4 = sem("top_sums")
        s_r4 = sem("top_reciprocals")
        s_sh = sem("logits_shifted")
        s_ex = sem("exps")
        s_mk = sem("masks")
        s_pr = sem("probs")
        s_pT = sem("pT_in_psum")
        s_pTs = sem("pT_in_sbuf")
        s_a = sem("attn_in_psum")
        s_ahi = sem("attn_hi")
        s_alo = sem("attn_lo")
        s_o = sem("attn_out_in_psum")
        s_an = sem("attn_out_normed")
        s_x2 = sem("residual_made")
        s_rn = sem("residual_normed")
        s_rT = sem("rT_in_psum")
        s_rThi = sem("rT_hi")
        s_rTlo = sem("rT_lo")
        s_gu = sem("gate_up_in_psum")
        s_th = sem("tanh_made")
        s_ga = sem("gate_made")
        s_h = sem("h_made")
        s_hhi = sem("h_hi")
        s_hlo = sem("h_lo")
        s_dn = sem("down_in_psum")
        s_dnn = sem("down_normed")
        s_y = sem("out_made")
        s_out = sem("out_stored")

        N_LB = HC + 2

        def after(eng, s, value):
            if not isinstance(value, int) or value > 0:
                eng.wait_ge(s, value)

        XT = LP[0][:, 0:KC * GT].rearrange("p (c n) -> p c n", c=KC)
        Q = LP[1][:, 0:KC * GT].rearrange("p (c n) -> p c n", c=KC)

        def has(g):
            return not isinstance(g, int) or 0 <= g < G

        LOOP = (1, G - 3)

        def tile_of(buffer, g, t):
            if isinstance(g, int):
                return buffer[:, NT * g + t, :]
            return buffer[:, bass.ds(NT * g + t, 1), :].rearrange("p a d -> p (a d)")

        block = ctx.enter_context(nc.Block())

        @block.sync
        def _(sp):
            xg = x_d.rearrange("(g t p) d -> g p t d", p=P, t=NT)
            sp.dma_start(x[:, 0:NT, :], xg[0]).then_inc(s_x0, 16)
            sp.dma_start(w32[:, 0, :, :], wq_d.rearrange("(c p) n -> p c n", p=P)).then_inc(s_w, 16)
            sp.dma_start(bqv[:, 0, :], bq_d).then_inc(s_w, 16)
            sp.dma_start(bqv[:, 1, :], bv_d).then_inc(s_w, 16)
            sp.wait_ge(s_pad, 1)
            for h in range(HC):
                sp.dma_start(lb32[h * HD:(h + 1) * HD, :, h * L:(h + 1) * L],
                             latT_d.rearrange("(c h d) l -> h d c l", c=KC, h=HC)[h]).then_inc(s_lb, 16)
            for e in range(2):
                sp.dma_start(lw[e * L:(e + 1) * L, :, e * HD:(e + 1) * HD],
                             lat_d.rearrange("l (j e d) -> e l j d", e=2, d=HD)[e]).then_inc(s_lb, 16)
            sp.dma_start(w32[:, 1, :, :], wv_d.rearrange("(c p) n -> p c n", p=P)).then_inc(s_w, 16)
            sp.dma_start(w32[:, 2, :, :], wo_d.rearrange("(c p) n -> p c n", p=P)).then_inc(s_w, 16)
            sp.dma_start(bo32[:, :], bo_d.rearrange("(a n) -> a n", a=1)).then_inc(s_w, 16)
            for g in range(1, G):
                sp.dma_start(x[:, g * NT:(g + 1) * NT, :], xg[g]).then_inc(s_xr, 16)

            def store(g):
                sp.wait_ge(s_y, g + 1)
                sp.dma_start(out_d[bass.ds(g * GT, GT), :].rearrange("(t p) d -> p t d", p=P), y[:, :, :])\
                  .then_inc(s_out, 16)

            with sp.Fori(0, G) as g:
                store(g)
            sp.wait_ge(s_out, 16 * (G + 1))

        @block.tensor
        def _(pe):
            def split3(out, lhs, rhs, first, last, skip=False):
                (lh, ll), (rh, rl) = lhs, rhs
                pe.matmul(out, lh, rh, start=first, stop=False, skip_group_check=skip)
                pe.matmul(out, lh, rl, start=False, stop=False, skip_group_check=skip)
                return pe.matmul(out, ll, rh, start=False, stop=last, skip_group_check=skip)

            def turn(out, src, done):
                for t in range(NT):
                    for c in range(KC):
                        last = pe.transpose(out[:, c, t * P:(t + 1) * P], src[:, t, c * P:(c + 1) * P], ident[:, :])
                last.then_inc(done, 1)

            def turn_x(g):
                pe.wait_ge(s_xn, g + 1)
                turn(XT, xn, s_xT)

            def turn_residual(g):
                pe.wait_ge(s_rn, g + 1)
                turn(GU[1], rn, s_rT)

            def q(g):
                pe.wait_ge(s_xThi, g + 1)
                pe.wait_ge(s_xTlo, g + 1)
                for m in range(KC):
                    for c in range(KC):
                        last = split3(Q[:, m, :],
                                      [w[:, 0, c, m * P:(m + 1) * P] for w in (whi, wlo)],
                                      [w[:, c, :] for w in (xThi, xTlo)], c == 0, c == KC - 1)
                last.then_inc(s_q, 1)

            def v(g):
                for m in range(KC):
                    for c in range(KC):
                        split3(X[:, m, :], [w[:, 1, c, m * P:(m + 1) * P] for w in (whi, wlo)],
                               [w[:, c, :] for w in (xThi, xTlo)], m == 0 and c == 0, False, skip=True)

            def logits(g, t):
                if t == 0:
                    pe.wait_ge(s_qhi, g + 1)
                    pe.wait_ge(s_qlo, g + 1)
                for c in range(KC):
                    last = split3(LP[t][:, c * HC * L:(c + 1) * HC * L],
                                  [w[:, c, t * P:(t + 1) * P] for w in (qhi, qlo)],
                                  [w[:, c, :] for w in (lbhi, lblo)], True, True)
                last.then_inc(s_l, 1)

            def turn_probs(g, t):
                pe.wait_ge(s_pr, NT * g + t + 1)
                if has(g + 1):
                    pe.wait_ge(s_lg, NT * (g + 1) + t + 1)
                for j in range(J):
                    last = pe.transpose(LP[t][:, j * P:(j + 1) * P],
                                        pr[t][:, 2 * j:2 * j + 2, :].rearrange("p h l -> p (h l)"), ident[:, :])
                last.then_inc(s_pT, 1)

            def weigh(g):
                pe.wait_ge(s_pTs, NT * g + NT)
                for j in range(J):
                    r, m = 32 * (j % 4), j // 4
                    last = pe.matmul(X[r:r + 2 * HD, m, :], lw[:, j, :], pT[:, j, :], start=False,
                                     stop=True, skip_group_check=True)
                last.then_inc(s_a, 1)

            def attn_out(g):
                pe.wait_ge(s_ahi, g + 1)
                pe.wait_ge(s_alo, g + 1)
                after(pe, s_dnn, g - 1)
                for t in range(NT):
                    pe.matmul(Y[:, t, :], ones[:, :], bohi[:, :], start=True, stop=False)
                    pe.matmul(Y[:, t, :], ones[:, :], bolo[:, :], start=False, stop=False)
                    for c in range(KC):
                        last = split3(Y[:, t, :], [w[:, c, t * P:(t + 1) * P] for w in (ahi, alo)],
                                      [w[:, 2, c, :] for w in (whi, wlo)], False, c == KC - 1)
                last.then_inc(s_o, 1)

            def gate_up(g, chunks):
                for f in chunks:
                    if f == 0:
                        pe.wait_ge(s_rThi, g + 1)
                        pe.wait_ge(s_rTlo, g + 1)
                    if f >= 2:
                        pe.wait_ge(s_h, NC * g + f - 1)
                    if f < FC:
                        for u in range(2):
                            for c in range(KC):
                                at = c * GUW + (2 * f + u) * P
                                last = split3(GU[f % 2][:, u, :], [w[:, at:at + P] for w in (fhi, flo)],
                                              [w[:, c, :] for w in (rThi, rTlo)], c == 0, c == KC - 1)
                    else:
                        for c in range(KC):
                            at = c * GUW + 2 * FC * P
                            last = split3(GU[f % 2][:, 0, :], [w[:, at:at + P] for w in (fhi, flo)],
                                          [w[:, c, :] for w in (rThi, rTlo)], c == 0, c == KC - 1)
                    last.then_inc(s_gu, 1)

            def down(g):
                if has(g + 1):
                    pe.wait_ge(s_an, g + 2)
                for f in range(NC):
                    rows = P if f < FC else TAIL
                    pe.wait_ge(s_hhi, NC * g + f + 1)
                    pe.wait_ge(s_hlo, NC * g + f + 1)
                    at = KC * GUW + f * D
                    for t in range(NT):
                        last = split3(Y[:, t, :], [w[0:rows, f, t * P:(t + 1) * P] for w in (hhi, hlo)],
                                      [w[0:rows, at:at + D] for w in (fhi, flo)], f == 0 and t == 0, f == NC - 1,
                                      skip=True)
                last.then_inc(s_dn, 1)

            def body(n):
                ffn, attn, tops, front = has(n), has(n + 1), has(n + 2), has(n + 3)
                done = has(n - 1)
                if ffn:
                    turn_residual(n)
                if attn:
                    turn_probs(n + 1, 0)
                if ffn:
                    gate_up(n, [0])
                if attn:
                    turn_probs(n + 1, 1)
                    weigh(n + 1)
                if ffn:
                    gate_up(n, [1])
                if attn:
                    attn_out(n + 1)
                if tops:
                    v(n + 2)
                if ffn:
                    gate_up(n, [2])
                if front:
                    turn_x(n + 3)
                if ffn:
                    gate_up(n, [3])
                if front:
                    q(n + 3)
                if ffn:
                    gate_up(n, [4])
                if front:
                    logits(n + 3, 0)
                if ffn:
                    gate_up(n, [5])
                if front:
                    logits(n + 3, 1)
                if ffn:
                    down(n)

            pe.wait_ge(s_cst, 2)
            pe.wait_ge(s_whi, 5)
            pe.wait_ge(s_wlo, 5)
            pe.wait_ge(s_lb, 16 * N_LB)
            def spread_indices(i):
                end = next(n for n, e in enumerate(IDX_ENDS) if (i + 1) * PW <= e)
                pe.wait_ge(s_ib, end + 1)
                if i >= 2:
                    pe.wait_ge(s_rc, i - 1)
                for b in range(NB):
                    last = pe.matmul(LP[i % 2][:, b * PW:(b + 1) * PW], spread[:, b, :, :].rearrange("p v r -> p (v r)"),
                                     idxb[:, i * PW:(i + 1) * PW], start=True, stop=True)
                last.then_inc(s_rp, 1)

            def look_up(i):
                if i >= 2:
                    pe.wait_ge(s_fhi, i - 1)
                    pe.wait_ge(s_flo, i - 1)
                for q in range(STEPS):
                    pe.wait_ge(s_hot, STEPS * i + q + 1)
                    for p in range(PARTS):
                        for b in range(NB):
                            last = pe.matmul(GU[i % 2][b * RB:(b + 1) * RB, 0, :], pick[:, q, p, :],
                                             hot[:, q, b * PW:(b + 1) * PW], start=q == 0 and p == 0,
                                             stop=q == STEPS - 1 and p == PARTS - 1, skip_group_check=True)
                    last.then_inc(s_used, 1)

            def ffn_weights(a, b):
                spread_indices(a)
                for i in range(a, b):
                    if i + 1 < b:
                        spread_indices(i + 1)
                    look_up(i)

            for n in range(-3, 0):
                body(n)
                if n == -3:
                    pe.wait_ge(s_pick, 2)
                pe.wait_ge(s_lg, NT * (n + 4))
                ffn_weights(*PHASES[n + 3])
            pe.wait_ge(s_fhi, PIECES)
            pe.wait_ge(s_flo, PIECES)
            body(0)
            with pe.Fori(*LOOP) as n:
                body(n)
            for n in range(LOOP[1], G + 1):
                body(n)

        @block.scalar
        def _(act):
            act.dma_start(lut[:, :], lut_d.rearrange("(a n) -> a n", a=1).broadcast_to([P, LUT])).then_inc(s_v, 16)
            act.wait_ge(s_pad, 3)
            for c in range(KC):
                at = c * GUW
                pair = idx[:, at:at + 2 * FC * P].rearrange("p (f u n) -> p f u n", u=2, n=P)
                for u, src in ((0, gi_d), (1, ui_d)):
                    rows = src[c * P:(c + 1) * P, :]
                    act.dma_start(pair[:, :, u, :], rows[:, 0:FC * P].rearrange("p (f n) -> p f n", n=P))\
                       .then_inc(s_i[c], 16)
                    act.dma_start(idx[:, at + 2 * FC * P + u * TU:at + 2 * FC * P + u * TU + TAIL],
                                  rows[:, FC * P:INTER]).then_inc(s_i[c], 16)
            at = KC * GUW
            act.dma_start(idx[:, at:at + FC * D].rearrange("p (f n) -> p f n", n=D),
                          di_d[0:FC * P, :].rearrange("(f p) n -> p f n", p=P)).then_inc(s_i[KC], 16)
            act.dma_start(idx[0:TAIL, at + FC * D:at + NC * D], di_d[FC * P:INTER, :]).then_inc(s_i[KC], 16)

            def apply(k, dst, src, g, done):
                act.wait_ge(s_nb[k], g + 1)
                for t in range(NT):
                    last = act.activation(dst[:, t, :], src(t), ACT.Identity, bias=nb[k][:, t:t + 1],
                                          scale=rstd[k][:, t:t + 1])
                last.then_inc(done, 1)

            def norm_x(g):
                apply("x", xn, lambda t: tile_of(x, g, t), g, s_xn)

            def xT(g):
                act.wait_ge(s_xT, g + 1)
                act.activation(xThi[:, :, :], XT, ACT.Copy).then_inc(s_xThi, 1)

            def q(g):
                act.wait_ge(s_q, g + 1)
                for m in range(KC):
                    last = act.activation(qhi[:, m, :], Q[:, m, :], ACT.Identity, bias=bqv[:, 0, m:m + 1])
                last.then_inc(s_qhi, 1)

            def logits(g, t):
                act.wait_ge(s_l, NT * g + t + 1)
                if has(g - 1):
                    act.wait_ge(s_marked, NT * (g - 1) + t + 1)
                    act.wait_ge(s_sh, NT * (g - 1) + t + 1)
                act.activation(lg[t][:, :, 0:L], LP[t][:, :].rearrange("p (h l) -> p h l", l=L), ACT.Copy)\
                   .then_inc(s_lg, 1)

            def exps(g, t):
                act.wait_ge(s_sh, NT * g + t + 1)
                act.activation(pr[t][:, :, :], pr[t][:, :, :], ACT.Exp, scale=HD ** -0.5).then_inc(s_ex, 1)

            def top_exps(g, t):
                act.wait_ge(s_e4, NT * g + t + 1)
                act.activation(w4[t][:, :, :], e4[t][:, :, :], ACT.Exp, scale=HD ** -0.5).then_inc(s_w4, 1)

            def probs_turned(g, t):
                act.wait_ge(s_pT, NT * g + t + 1)
                act.activation(pT[:, :, t * P:(t + 1) * P], LP[t][:, :].rearrange("p (j n) -> p j n", n=P), ACT.Copy)\
                   .then_inc(s_pTs, 1)

            def attn(g):
                act.wait_ge(s_a, g + 1)
                for m in range(KC):
                    last = act.activation(ahi[:, m, :], X[:, m, :], ACT.Identity, bias=bqv[:, 1, m:m + 1])
                last.then_inc(s_ahi, 1)

            def norm_attn(g):
                apply("a", an, lambda t: Y[:, t, :], g, s_an)

            def norm_residual(g):
                apply("r", rn, lambda t: tile_of(x, g, t), g, s_rn)

            def rT(g):
                act.wait_ge(s_rT, g + 1)
                act.activation(rThi[:, :, :], GU[1][:, :, :], ACT.Copy).then_inc(s_rThi, 1)

            def tanh(g, f):
                rows = P if f < FC else TAIL
                act.wait_ge(s_gu, NC * g + f + 1)
                act.activation(th[0:rows, f % 2, :], GU[f % 2][0:rows, 0, :], ACT.Tanh, scale=0.5).then_inc(s_th, 1)

            def h_hi(g, f):
                rows = P if f < FC else TAIL
                act.wait_ge(s_h, NC * g + f + 1)
                act.activation(hhi[0:rows, f, :], h32[0:rows, f % 2, :], ACT.Copy).then_inc(s_hhi, 1)

            def norm_down(g):
                apply("d", dn, lambda t: Y[:, t, :], g, s_dnn)

            act.wait_ge(s_w, 16 * 6)
            act.wait_ge(s_lb, 16 * N_LB)
            act.activation(lbhi[:, :, :], lb32[:, :, :], ACT.Copy).then_inc(s_whi, 1)
            for i in range(3):
                act.activation(whi[:, i, :, :], w32[:, i, :, :], ACT.Copy).then_inc(s_whi, 1)
            act.activation(bohi[:, :], bo32[:, :], ACT.Copy).then_inc(s_whi, 1)

            def copy_spread(i):
                if i == 0:
                    act.wait_ge(s_nv, NB)
                act.wait_ge(s_rp, i + 1)
                if i >= 2:
                    act.wait_ge(s_hot, STEPS * (i - 1))
                act.activation(rep[:, i % 2, :], LP[i % 2][:, :], ACT.Identity, bias=nv[:, :]).then_inc(s_rc, 1)

            def weights_hi(i):
                a = i * PW
                act.wait_ge(s_used, STEPS * (i + 1))
                act.activation(fhi[:, a:a + PW], GU[i % 2][:, 0, :], ACT.Copy, scale=1.0 if a < KC * GUW else 0.5)\
                   .then_inc(s_fhi, 1)

            def ffn_weights(a, b):
                copy_spread(a)
                for i in range(a, b):
                    if i + 1 < b:
                        copy_spread(i + 1)
                    weights_hi(i)

            def body(n):
                ffn, out, tops, front = has(n), has(n + 1), has(n + 2), has(n + 3)
                done = has(n - 1)
                if ffn:
                    rT(n)
                if out:
                    probs_turned(n + 1, 0)
                if done:
                    norm_down(n - 1)
                if ffn:
                    tanh(n, 0)
                if out:
                    probs_turned(n + 1, 1)
                    attn(n + 1)
                if front:
                    norm_x(n + 3)
                if tops:
                    top_exps(n + 2, 0)
                    exps(n + 2, 0)
                if ffn:
                    tanh(n, 1)
                    h_hi(n, 0)
                if out:
                    norm_attn(n + 1)
                if ffn:
                    tanh(n, 2)
                    h_hi(n, 1)
                if front:
                    xT(n + 3)
                if ffn:
                    tanh(n, 3)
                    h_hi(n, 2)
                if front:
                    q(n + 3)
                if tops:
                    top_exps(n + 2, 1)
                    exps(n + 2, 1)
                if ffn:
                    tanh(n, 4)
                    h_hi(n, 3)
                if front:
                    logits(n + 3, 0)
                if out:
                    norm_residual(n + 1)
                if ffn:
                    tanh(n, 5)
                    h_hi(n, 4)
                if front:
                    logits(n + 3, 1)
                if ffn:
                    h_hi(n, 5)

            body(-3)
            ffn_weights(*PHASES[0])
            body(-2)
            ffn_weights(*PHASES[1])
            body(-1)
            ffn_weights(*PHASES[2])
            body(0)
            with act.Fori(*LOOP) as n:
                body(n)
            for n in range(LOOP[1], G + 1):
                body(n)

        @block.vector
        def _(dve):
            def held(i):
                dve.memset(spare[:, i:i + 1], 0.0)

            def stats(k, src, g):
                for t in range(NT):
                    last = dve.bn_stats(st[k][:, t, :], src(t))
                last.then_inc(s_st[k], 1)
                dve.wait_ge(s_st[k], g + 1)
                held(KINDS.index(k))
                for t in range(NT):
                    last = dve.bn_aggr(mv[k][:, t, :], st[k][:, t, :])
                last.then_inc(s_mv[k], 1)
                dve.wait_ge(s_mv[k], g + 1)
                dve.tensor_scalar(ve[k][:, :], mv[k][:, :, 1], EPS, None, ALU.add)
                dve.tensor_scalar(nm[k][:, :], mv[k][:, :, 0], -1.0, None, ALU.mult).then_inc(s_ve[k], 1)

            def stats_x(g):
                stats("x", lambda t: tile_of(x, g, t), g)

            def stats_attn(g):
                dve.wait_ge(s_o, g + 1)
                stats("a", lambda t: Y[:, t, :], g)

            def stats_residual(g):
                dve.wait_ge(s_x2, g + 1)
                stats("r", lambda t: tile_of(x, g, t), g)

            def stats_down(g):
                dve.wait_ge(s_dn, g + 1)
                stats("d", lambda t: Y[:, t, :], g)

            def low(dst, src, hi, done):
                return dve.tensor_tensor(dst, src, hi.bitcast(F32), ALU.subtract).then_inc(done, 1)

            def xT(g):
                dve.wait_ge(s_xThi, g + 1)
                low(xTlo[:, :, :], XT, xThi[:, :, :], s_xTlo)

            def biased_low(dst, src, bias, hi):
                return dve.scalar_tensor_tensor(dst, src, bias, hi.bitcast(F32), ALU.add, ALU.subtract)

            def q(g):
                dve.wait_ge(s_qhi, g + 1)
                for m in range(KC):
                    last = biased_low(qlo[:, m, :], Q[:, m, :], bqv[:, 0, m:m + 1], qhi[:, m, :])
                last.then_inc(s_qlo, 1)

            def attn(g):
                dve.wait_ge(s_ahi, g + 1)
                for m in range(KC):
                    last = biased_low(alo[:, m, :], X[:, m, :], bqv[:, 1, m:m + 1], ahi[:, m, :])
                last.then_inc(s_alo, 1)

            def rT(g):
                dve.wait_ge(s_rThi, g + 1)
                low(rTlo[:, :, :], GU[1][:, :, :], rThi[:, :, :], s_rTlo)

            def top(g, t, a=0, b=H):
                if a == 0:
                    dve.wait_ge(s_lg, NT * g + t + 1)
                    held(len(KINDS) + t)
                for h in range(a, b):
                    last = dve.max(m8[t][:, h, :], lg[t][:, h, :])
                if b == H:
                    last.then_inc(s_top, 1)

            def mark(g, t, a=0, b=H):
                for h in range(a, b):
                    last = dve.match_replace(marked[t][:, h, :], m8[t][:, h, :], lg[t][:, h, :], MARK)
                if b == H:
                    last.then_inc(s_marked, 1)

            def shift_top(g, t):
                dve.wait_ge(s_top, NT * g + t + 1)
                dve.tensor_tensor(e4[t][:, :, :], m8[t][:, :, K_TOP:2 * K_TOP],
                                  m8[t][:, :, K_TOP:K_TOP + 1].broadcast_to([P, H, K_TOP]), ALU.subtract)\
                   .then_inc(s_e4, 1)

            def masks(g, t):
                dve.wait_ge(s_w4, NT * g + t + 1)
                dve.tensor_reduce(s4[t][:, :], w4[t][:, :, :], AX_X, ALU.add).then_inc(s_s4, 1)
                dve.wait_ge(s_s4, NT * g + t + 1)
                dve.reciprocal(r4[t][:, :], s4[t][:, :]).then_inc(s_r4, 1)
                dve.wait_ge(s_r4, NT * g + t + 1)
                dve.wait_ge(s_marked, NT * g + t + 1)
                dve.scalar_tensor_tensor(mk[t][:, :, :], marked[t][:, :, 0:L], MARK,
                                         r4[t][:, :].rearrange("p (h a) -> p h a", a=1).broadcast_to([P, H, L]),
                                         ALU.is_equal, ALU.mult).then_inc(s_mk, 1)

            def gate(g, f):
                rows, at, u = (P, 0, 1) if f < FC else (TAIL, TU, 0)
                dve.wait_ge(s_th, NC * g + f + 1)
                dve.scalar_tensor_tensor(ga[0:rows, f % 2, :], th[0:rows, f % 2, :], 1.0, GU[f % 2][0:rows, 0, :],
                                         ALU.add, ALU.mult).then_inc(s_ga, 1)
                dve.wait_ge(s_ga, NC * g + f + 1)
                if f >= 2:
                    dve.wait_ge(s_hhi, NC * g + f - 1)
                    dve.wait_ge(s_hlo, NC * g + f - 1)
                dve.tensor_tensor(h32[0:rows, f % 2, :], ga[0:rows, f % 2, :],
                                  GU[f % 2][at:at + rows, u, :], ALU.mult).then_inc(s_h, 1)

            dve.wait_ge(s_x0, 16)
            stats_x(0)
            dve.wait_ge(s_whi, 1)
            low(lblo[:, :, :], lb32[:, :, :], lbhi[:, :, :], s_wlo)
            for i in range(3):
                dve.wait_ge(s_whi, i + 2)
                low(wlo[:, i, :, :], w32[:, i, :, :], whi[:, i, :, :], s_wlo)
            dve.wait_ge(s_whi, 5)
            low(bolo[:, :], bo32[:, :], bohi[:, :], s_wlo)
            dve.wait_ge(s_v, 16)
            dve.wait_ge(s_eye, 1)
            for v in range(NB):
                rows = slice(v * RB, (v + 1) * RB)
                dve.tensor_copy(eye32[rows, :], eye[rows, rows]).then_inc(s_e32, 1)
                dve.memset(nv[rows, :], -float(v)).then_inc(s_nv, 1)
            for v in range(NB):
                rows = slice(v * RB, (v + 1) * RB)
                dve.tensor_copy(vlut[rows, :], lut[rows, :].rearrange("p (s v) -> p v s", v=NB)[:, v, :])\
                   .then_inc(s_vl, 1)
            dve.wait_ge(s_vl, NB)
            dve.tensor_copy(parts[:, :, 0], vlut[:, :]).then_inc(s_part, 1)
            dve.wait_ge(s_part, 1)
            dve.tensor_tensor(rest[:, 0, :], vlut[:, :], parts[:, :, 0], ALU.subtract).then_inc(s_part, 1)
            dve.wait_ge(s_part, 2)
            dve.tensor_copy(parts[:, :, 1], rest[:, 0, :]).then_inc(s_part, 1)
            dve.wait_ge(s_part, 3)
            dve.tensor_tensor(rest[:, 1, :], rest[:, 0, :], parts[:, :, 1], ALU.subtract).then_inc(s_part, 1)
            dve.wait_ge(s_part, 4)
            dve.tensor_copy(parts[:, :, 2], rest[:, 1, :]).then_inc(s_part, 1)

            def one_hot(i):
                dve.wait_ge(s_rc, i + 1)
                for q in range(STEPS):
                    if i:
                        dve.wait_ge(s_used, STEPS * (i - 1) + q + 1)
                    dve.tensor_scalar(hot[:, q, :], rep[:, i % 2, :], float(NB * q), None, ALU.is_equal)\
                       .then_inc(s_hot, 1)

            def weights_lo(i):
                a = i * PW
                dve.wait_ge(s_fhi, i + 1)
                dve.scalar_tensor_tensor(flo[:, a:a + PW], GU[i % 2][:, 0, :], 1.0 if a < KC * GUW else 0.5,
                                         fhi[:, a:a + PW].bitcast(F32), ALU.mult, ALU.subtract).then_inc(s_flo, 1)

            def ffn_weights(a, b):
                one_hot(a)
                for i in range(a, b):
                    if i + 1 < b:
                        one_hot(i + 1)
                    weights_lo(i)

            def body(n):
                ffn, out, tops, front = has(n), has(n + 1), has(n + 2), has(n + 3)
                done = has(n - 1)
                if ffn:
                    rT(n)
                if done:
                    stats_down(n - 1)
                if tops:
                    top(n + 2, 0)
                    shift_top(n + 2, 0)
                if front and not (isinstance(n, int) and n == -3):
                    stats_x(n + 3)
                if ffn:
                    gate(n, 0)
                if tops:
                    mark(n + 2, 0, 0, HC)
                if out:
                    attn(n + 1)
                if tops:
                    mark(n + 2, 0, HC, H)
                if ffn:
                    gate(n, 1)
                if tops:
                    masks(n + 2, 0)
                if out:
                    stats_attn(n + 1)
                if tops:
                    top(n + 2, 1, 0, HC)
                if ffn:
                    gate(n, 2)
                if front:
                    xT(n + 3)
                if tops:
                    top(n + 2, 1, HC, H)
                    shift_top(n + 2, 1)
                if ffn:
                    gate(n, 3)
                if front:
                    q(n + 3)
                if tops:
                    mark(n + 2, 1, 0, HC)
                if out:
                    stats_residual(n + 1)
                if ffn:
                    gate(n, 4)
                if tops:
                    mark(n + 2, 1, HC, H)
                if ffn:
                    gate(n, 5)
                if tops:
                    masks(n + 2, 1)

            body(-3)
            dve.wait_ge(s_xr, 16 * (G - 1))
            ffn_weights(*PHASES[0])
            body(-2)
            ffn_weights(*PHASES[1])
            body(-1)
            ffn_weights(*PHASES[2])
            body(0)
            with dve.Fori(*LOOP) as n:
                body(n)
            for n in range(LOOP[1], G + 1):
                body(n)

        @block.gpsimd
        def _(pool):
            pool.memset(lb32[:, :, :], 0.0)
            pool.memset(lw[:, :, :], 0.0).then_inc(s_pad, 1)
            for c in range(KC):
                pool.memset(idx[:, c * GUW + 2 * FC * P:(c + 1) * GUW], 0)
            pool.memset(idx[:, KC * GUW + FC * D:WALL], 0).then_inc(s_pad, 2)
            pool.memset(half[:, :], -0.5)
            pool.memset(ones[:, :].bitcast(F32), 1.0).then_inc(s_out, 16)
            for t in range(NT):
                pool.memset(lg[t][:, :, L:LROW], SENTINEL)
            pool.memset(ident[:, :], 0.0).then_inc(s_cst, 1)
            pool.wait_ge(s_cst, 1)
            pool.affine_select(out=ident[:, :], in_=ident[:, :], compare_op=ALU.not_equal, fill=1.0,
                               base=0, pattern=[[-1, P]], channel_multiplier=1).then_inc(s_cst, 1)
            pool.wait_ge(s_cst, 2)

            def rstds(k, g):
                pool.wait_ge(s_ve[k], g + 1)
                pool.tensor_tensor(rstd[k][:, :], ve[k][:, :], half[:, :], ALU.pow).then_inc(s_rs[k], 1)
                pool.wait_ge(s_rs[k], g + 1)
                pool.tensor_tensor(nb[k][:, :], nm[k][:, :], rstd[k][:, :], ALU.mult).then_inc(s_nb[k], 1)

            def rows_of(g):
                return x[:, NT * g:NT * g + NT, :] if isinstance(g, int) else x[:, bass.ds(NT * g, NT), :]

            def residual(g):
                pool.wait_ge(s_an, g + 1)
                pool.tensor_tensor(rows_of(g), an[:, :, :], rows_of(g), ALU.add).then_inc(s_x2, 1)

            def shift(g, t):
                pool.wait_ge(s_top, NT * g + t + 1)
                if has(g - 1):
                    pool.wait_ge(s_pT, NT * (g - 1) + t + 1)
                pool.tensor_tensor(pr[t][:, :, :], lg[t][:, :, 0:L],
                                   m8[t][:, :, K_TOP:K_TOP + 1].broadcast_to([P, H, L]), ALU.subtract)\
                    .then_inc(s_sh, 1)

            def probs(g, t):
                pool.wait_ge(s_ex, NT * g + t + 1)
                pool.wait_ge(s_mk, NT * g + t + 1)
                pool.tensor_tensor(pr[t][:, :, :], pr[t][:, :, :], mk[t][:, :, :], ALU.mult).then_inc(s_pr, 1)

            def h_lo(g, f):
                rows = P if f < FC else TAIL
                pool.wait_ge(s_hhi, NC * g + f + 1)
                pool.tensor_tensor(hlo[0:rows, f, :], h32[0:rows, f % 2, :], hhi[0:rows, f, :].bitcast(F32),
                                   ALU.subtract).then_inc(s_hlo, 1)

            def output(g):
                pool.wait_ge(s_dnn, g + 1)
                pool.wait_ge(s_out, 16 * (g + 1))
                pool.tensor_tensor(y[:, :, :], dn[:, :, :], rows_of(g), ALU.add).then_inc(s_y, 1)

            def body(n):
                ffn, out, tops, front = has(n), has(n + 1), has(n + 2), has(n + 3)
                done = has(n - 1)
                if done:
                    rstds("d", n - 1)
                if tops:
                    shift(n + 2, 0)
                if front:
                    rstds("x", n + 3)
                if done:
                    output(n - 1)
                if ffn:
                    h_lo(n, 0)
                if out:
                    rstds("a", n + 1)
                if tops:
                    probs(n + 2, 0)
                if out:
                    residual(n + 1)
                if ffn:
                    h_lo(n, 1)
                    h_lo(n, 2)
                if tops:
                    shift(n + 2, 1)
                if out:
                    rstds("r", n + 1)
                if ffn:
                    h_lo(n, 3)
                    h_lo(n, 4)
                    h_lo(n, 5)
                if tops:
                    probs(n + 2, 1)

            pool.tensor_copy(eye[:, :], ident[:, :]).then_inc(s_eye, 1)
            pool.wait_ge(s_eye, 1)
            pool.tensor_copy(spread[:, :, :, :],
                             eye[:, :].rearrange("p (b a r) -> p b a r", b=NB, a=1).broadcast_to([P, NB, NB, RB]))\
                .then_inc(s_eye, 1)
            pool.wait_ge(s_eye, 2)
            body(-3)
            pool.wait_ge(s_part, 5)
            pool.wait_ge(s_e32, NB)
            pool.tensor_tensor(pick[:, :, :, :].rearrange("p q t r -> p (q t) r"),
                               eye32[:, :].rearrange("p (a r) -> p a r", a=1).broadcast_to([P, STEPS * PARTS, RB]),
                               parts[:, :, :].rearrange("p q (t a) -> p (q t) a", a=1)
                               .broadcast_to([P, STEPS * PARTS, RB]), ALU.mult).then_inc(s_pick, 2)
            for i, end in enumerate(IDX_ENDS):
                pool.wait_ge(s_i[i], 16 * (4 if i < KC else 2))
                at = IDX_ENDS[i - 1] if i else 0
                pool.tensor_copy(idxb[:, at:end], idx[:, at:end]).then_inc(s_ib, 1)
            for n in range(-2, LOOP[0]):
                body(n)
            with pool.Fori(*LOOP) as n:
                body(n)
            for n in range(LOOP[1], G + 1):
                body(n)


def kernel(**inputs):
    import numpy as np
    import concourse.bacc as bacc
    from concourse.bass_utils import run_bass_kernel_spmd

    def a(name):
        return np.asarray(inputs[name])

    lay = np.ascontiguousarray
    arrays = {
        "x_in": lay(a("L0_attn_hidden_states")[0]),
        "wq_in": lay(a("L0_attn_Wq").T), "bq_in": lay(a("L0_attn_bq").reshape(KC, P).T),
        "wv_in": lay(a("L0_attn_Wv").T), "bv_in": lay(a("L0_attn_bv").reshape(KC, P).T),
        "wo_in": lay(a("L0_attn_Wo").T), "bo_in": lay(a("L0_attn_bo")),
        "lat_in": lay(a("L0_attn_latent_keys")), "latT_in": lay(a("L0_attn_latent_keys").T),
        "lut_in": lay(a("L0_ffn_lut")),
        "gate_in": lay(a("L0_ffn_gate_idx").T), "up_in": lay(a("L0_ffn_up_idx").T),
        "down_in": lay(a("L0_ffn_down_idx").T),
    }
    nc = bacc.Bacc("TRN2", target_bir_lowering=False, num_devices=1)
    args = [nc.dram_tensor(n, v.shape, mybir.dt.from_np(v.dtype), kind="ExternalInput").ap() for n, v in arrays.items()]
    out = nc.dram_tensor("out", (T, D), F32, kind="ExternalOutput").ap()
    build(nc, *args, out)
    r = run_bass_kernel_spmd(nc, [arrays], core_ids=[0])
    return r.results[0]["out"].reshape(1, T, D)
```

```python
from contextlib import ExitStack

import concourse.bass as bass
from concourse import mybir

F32 = mybir.dt.float32
F32R = mybir.dt.float32r
BF16 = mybir.dt.bfloat16
I32 = mybir.dt.int32
ALU = mybir.AluOpType
ACT = mybir.ActivationFunctionType
AX_X = mybir.AxisListType.X

P = 128
T = 2048
D = 256
H = 16
HD = D // H
L = 64
K_TOP = 4
INTER = 688
LUT = 16
EPS = 1e-5

KC = D // P
NT = 2
G = T // (NT * P)
GT = NT * P
HC = H // KC
J = H * L // P
LROW = L + K_TOP
FC = INTER // P
TAIL = INTER - FC * P
TU = 64
NC = FC + 1
GUW = FC * 2 * P + P
WALL = KC * GUW + NC * D
SENTINEL = 3.0e38
MARK = -3.0e38
PW = 512
PIECES = [(a, min(PW, WALL - a)) for a in range(0, WALL, PW)]
RB = 32
NB = P // RB
STEPS = LUT // NB
PARTS = 3
IDX_ENDS = [(c + 1) * GUW for c in range(KC)] + [WALL]
EARLY = 2
PLACES = {-2: {0: [2], 1: [3], 2: [4], 3: [5]}, -1: {0: [6, 7, 8]}}


def build(nc, x_d, wq_d, bq_d, wv_d, bv_d, wo_d, bo_d, lat_d, latT_d, lut_d, gi_d, ui_d, di_d, out_d):
    ctx = ExitStack()
    with ctx:
        def sb(name, shape, dt=F32):
            return ctx.enter_context(nc.sbuf_tensor(name, shape, dt))

        def sem(name):
            return ctx.enter_context(nc.semaphore(name))

        x = sb("x", [P, G * NT, D])
        ident = sb("ident", [P, P])
        half = sb("half", [P, NT])
        spare = sb("spare", [P, 8])
        ones = sb("ones", [1, P], F32R)
        pT = sb("pT", [P, J, GT])
        w32 = pT[:, 0:3 * KC, :].rearrange("p (i c) n -> p i c n", c=KC)
        whi = sb("whi", [P, 3, KC, D], F32R)
        wlo = sb("wlo", [P, 3, KC, D], F32R)
        bqv = sb("bqv", [P, 2, KC])
        bo32 = sb("bo32", [1, D])
        bohi = sb("bohi", [1, D], F32R)
        bolo = sb("bolo", [1, D], F32R)
        late = sb("late", [P, 2 * NT, D])
        dn, y = late[:, 0:NT, :], late[:, NT:2 * NT, :]
        lb32 = late[:, :, :].rearrange("p (c t) d -> p c (t d)", c=KC)
        lbhi = sb("lbhi", [P, KC, HC * L], F32R)
        lblo = sb("lblo", [P, KC, HC * L], F32R)
        lw = sb("lw", [P, J, 2 * HD])
        lut = sb("lut", [P, LUT])
        vlut = sb("vlut", [P, STEPS])
        nv = sb("nv", [P, 1])
        rest = sb("rest", [P, 2, STEPS])
        parts = sb("parts", [P, STEPS, PARTS], BF16)
        eye = sb("eye", [P, P], BF16)
        eye32 = sb("eye32", [P, RB], BF16)
        pick = sb("pick", [P, STEPS, PARTS, RB], BF16)
        spread = sb("spread", [P, NB, NB, RB], BF16)
        idx = sb("idx", [P, WALL], I32)
        idxb = sb("idxb", [P, WALL], BF16)
        gates = sb("gates", [P, 3, 2, GT])
        th, ga, h32 = (gates[:, i, :, :] for i in range(3))
        normed = sb("normed", [P, 2, NT, D])
        an, rn = normed[:, 0, :, :], normed[:, 1, :, :]
        rep = [b.rearrange("p a u n -> p (a u n)").bitcast(BF16).rearrange("p (b n) -> p b n", b=NB)
               for b in (gates[:, 0:2, :, :], normed[:, :, :, :])]
        hot = sb("hot", [P, STEPS, NB, PW], BF16)
        fhi = sb("fhi", [P, WALL], F32R)
        flo = sb("flo", [P, WALL], F32R)

        KINDS = ("x", "a", "r", "d")
        st = {k: sb(f"st_{k}", [P, NT, 6]) for k in KINDS}
        mv = {k: sb(f"mv_{k}", [P, NT, 2]) for k in KINDS}
        ve = {k: sb(f"ve_{k}", [P, NT]) for k in KINDS}
        nm = {k: sb(f"nm_{k}", [P, NT]) for k in KINDS}
        rstd = {k: sb(f"rstd_{k}", [P, NT]) for k in KINDS}
        nb = {k: sb(f"nb_{k}", [P, NT]) for k in KINDS}

        xn = sb("xn", [P, NT, D])
        xThi = sb("xThi", [P, KC, GT], F32R)
        xTlo = sb("xTlo", [P, KC, GT], F32R)
        qhi = sb("qhi", [P, KC, GT], F32R)
        qlo = sb("qlo", [P, KC, GT], F32R)
        lg = [sb(f"lg{t}", [P, H, LROW]) for t in range(NT)]
        marked = [sb(f"marked{t}", [P, H, LROW]) for t in range(NT)]
        m8 = [sb(f"m8_{t}", [P, H, 8]) for t in range(NT)]
        e4 = [sb(f"e4_{t}", [P, H, K_TOP]) for t in range(NT)]
        w4 = [sb(f"w4_{t}", [P, H, K_TOP]) for t in range(NT)]
        s4 = [sb(f"s4_{t}", [P, H]) for t in range(NT)]
        r4 = [sb(f"r4_{t}", [P, H]) for t in range(NT)]
        pr = [sb(f"pr{t}", [P, H, L]) for t in range(NT)]
        mk = [sb(f"mk{t}", [P, H, L]) for t in range(NT)]
        ahi = sb("ahi", [P, KC, GT], F32R)
        alo = sb("alo", [P, KC, GT], F32R)
        rThi = sb("rThi", [P, KC, GT], F32R)
        rTlo = sb("rTlo", [P, KC, GT], F32R)
        hhi = sb("hhi", [P, NC, GT], F32R)
        hlo = sb("hlo", [P, NC, GT], F32R)

        LP = [ctx.enter_context(nc.psum_tensor(f"LP{t}", [P, H * L], F32)) for t in range(NT)]
        GU = [ctx.enter_context(nc.psum_tensor(f"GU{i}", [P, 2, GT], F32)) for i in range(2)]
        X = ctx.enter_context(nc.psum_tensor("X", [P, KC, GT], F32))
        Y = ctx.enter_context(nc.psum_tensor("Y", [P, NT, D], F32))

        s_x0 = sem("x_first_loaded")
        s_x1 = sem("x_second_loaded")
        s_xr = sem("x_rest_loaded")
        s_w = sem("wq_loaded")
        s_w2 = sem("wv_wo_loaded")
        s_lb = sem("latent_blocks_loaded")
        s_lw = sem("latents_loaded")
        s_i = [sem(f"indices_loaded_{i}") for i in range(len(IDX_ENDS))]
        s_v = sem("lut_loaded")
        s_pad = sem("pads_cleared")
        s_cst = sem("constants_made")
        s_whi = sem("weights_hi_made")
        s_wlo = sem("weights_lo_made")
        s_eye = sem("bf16_identities_made")
        s_e32 = sem("block_identity_made")
        s_nv = sem("partition_values_made")
        s_vl = sem("lut_by_partition")
        s_part = sem("lut_parts_made")
        s_pick = sem("lookup_stationaries_made")
        s_ib = sem("indices_in_bf16")
        s_rp = sem("indices_spread_in_psum")
        s_rc = sem("indices_spread")
        s_hot = sem("one_hot_made")
        s_used = sem("one_hot_used")
        s_fhi = sem("ffn_weights_hi_made")
        s_flo = sem("ffn_weights_lo_made")
        s_st = {k: sem(f"stats_{k}") for k in KINDS}
        s_mv = {k: sem(f"moments_{k}") for k in KINDS}
        s_ve = {k: sem(f"var_eps_{k}") for k in KINDS}
        s_rs = {k: sem(f"rstd_{k}_made") for k in KINDS}
        s_nb = {k: sem(f"ln_bias_{k}") for k in KINDS}
        s_xn = sem("xn_made")
        s_xT = sem("xT_in_psum")
        s_xThi = sem("xT_hi")
        s_xTlo = sem("xT_lo")
        s_q = sem("q_in_psum")
        s_qhi = sem("q_hi")
        s_qlo = sem("q_lo")
        s_l = sem("logits_in_psum")
        s_lg = sem("logits_in_sbuf")
        s_top = sem("top_found")
        s_marked = sem("top_marked")
        s_e4 = sem("top_shifted")
        s_w4 = sem("top_exps")
        s_s4 = sem("top_sums")
        s_r4 = sem("top_reciprocals")
        s_sh = sem("logits_shifted")
        s_ex = sem("exps")
        s_mk = sem("masks")
        s_pr = sem("probs")
        s_pT = sem("pT_in_psum")
        s_pTs = sem("pT_in_sbuf")
        s_a = sem("attn_in_psum")
        s_ahi = sem("attn_hi")
        s_alo = sem("attn_lo")
        s_o = sem("attn_out_in_psum")
        s_an = sem("attn_out_normed")
        s_x2 = sem("residual_made")
        s_rn = sem("residual_normed")
        s_rT = sem("rT_in_psum")
        s_rThi = sem("rT_hi")
        s_rTlo = sem("rT_lo")
        s_gu = sem("gate_up_in_psum")
        s_th = sem("tanh_made")
        s_ga = sem("gate_made")
        s_h = sem("h_made")
        s_hhi = sem("h_hi")
        s_hlo = sem("h_lo")
        s_dn = sem("down_in_psum")
        s_dnn = sem("down_normed")
        s_y = sem("out_made")
        s_out = sem("out_stored")

        N_WQ, N_LB, N_WV, N_WO, N_BO = 1, 2, 3, 4, 5

        def after(eng, s, value):
            if not isinstance(value, int) or value > 0:
                eng.wait_ge(s, value)

        XT = LP[0][:, 0:KC * GT].rearrange("p (c n) -> p c n", c=KC)
        Q = LP[1][:, 0:KC * GT].rearrange("p (c n) -> p c n", c=KC)

        def has(g):
            return not isinstance(g, int) or 0 <= g < G

        def pieces_at(n, place):
            return PLACES[n].get(place, []) if isinstance(n, int) and n in PLACES else []

        LOOP = (1, G - 3)

        def tile_of(buffer, g, t):
            if isinstance(g, int):
                return buffer[:, NT * g + t, :]
            return buffer[:, bass.ds(NT * g + t, 1), :].rearrange("p a d -> p (a d)")

        block = ctx.enter_context(nc.Block())

        @block.sync
        def _(sp):
            xg = x_d.rearrange("(g t p) d -> g p t d", p=P, t=NT)
            sp.dma_start(x[:, 0:NT, :], xg[0]).then_inc(s_x0, 16)
            sp.dma_start(lut[:, :], lut_d.rearrange("(a n) -> a n", a=1).broadcast_to([P, LUT])).then_inc(s_v, 16)
            sp.wait_ge(s_pad, 3)

            def load_gate_up(c):
                at = c * GUW
                pair = idx[:, at:at + 2 * FC * P].rearrange("p (f u n) -> p f u n", u=2, n=P)
                for u, src in ((0, gi_d), (1, ui_d)):
                    rows = src[c * P:(c + 1) * P, :]
                    sp.dma_start(pair[:, :, u, :], rows[:, 0:FC * P].rearrange("p (f n) -> p f n", n=P))\
                      .then_inc(s_i[c], 16)
                    sp.dma_start(idx[:, at + 2 * FC * P + u * TU:at + 2 * FC * P + u * TU + TAIL],
                                 rows[:, FC * P:INTER]).then_inc(s_i[c], 16)

            load_gate_up(0)
            sp.dma_start(w32[:, 0, :, :], wq_d.rearrange("(c p) n -> p c n", p=P)).then_inc(s_w, 16)
            sp.dma_start(bqv[:, 0, :], bq_d).then_inc(s_w, 16)
            for h in range(HC):
                sp.dma_start(lb32[h * HD:(h + 1) * HD, :, h * L:(h + 1) * L],
                             latT_d.rearrange("(c h d) l -> h d c l", c=KC, h=HC)[h]).then_inc(s_lb, 16)
            load_gate_up(1)
            sp.dma_start(x[:, NT:2 * NT, :], xg[1]).then_inc(s_x1, 16)
            sp.dma_start(w32[:, 1, :, :], wv_d.rearrange("(c p) n -> p c n", p=P)).then_inc(s_w2, 16)
            sp.dma_start(w32[:, 2, :, :], wo_d.rearrange("(c p) n -> p c n", p=P)).then_inc(s_w2, 16)
            sp.dma_start(bqv[:, 1, :], bv_d).then_inc(s_w2, 16)
            sp.dma_start(bo32[:, :], bo_d.rearrange("(a n) -> a n", a=1)).then_inc(s_w2, 16)
            at = KC * GUW
            sp.dma_start(idx[:, at:at + FC * D].rearrange("p (f n) -> p f n", n=D),
                         di_d[0:FC * P, :].rearrange("(f p) n -> p f n", p=P)).then_inc(s_i[KC], 16)
            sp.dma_start(idx[0:TAIL, at + FC * D:at + NC * D], di_d[FC * P:INTER, :]).then_inc(s_i[KC], 16)
            for e in range(2):
                sp.dma_start(lw[e * L:(e + 1) * L, :, e * HD:(e + 1) * HD],
                             lat_d.rearrange("l (j e d) -> e l j d", e=2, d=HD)[e]).then_inc(s_lw, 16)
            for g, n in ((2, 2), (4, G - 4)):
                sp.dma_start(x[:, g * NT:(g + n) * NT, :].rearrange("p (g t) d -> p g t d", t=NT),
                             x_d.rearrange("(g t p) d -> p g t d", p=P, t=NT)[:, g:g + n]).then_inc(s_xr, 16)

            def store(g):
                sp.wait_ge(s_y, g + 1)
                sp.dma_start(out_d[bass.ds(g * GT, GT), :].rearrange("(t p) d -> p t d", p=P), y[:, :, :])\
                  .then_inc(s_out, 16)

            with sp.Fori(0, G) as g:
                store(g)
            sp.wait_ge(s_out, 16 * (G + 1))

        @block.tensor
        def _(pe):
            def split3(out, lhs, rhs, first, last, skip=False):
                (lh, ll), (rh, rl) = lhs, rhs
                pe.matmul(out, lh, rh, start=first, stop=False, skip_group_check=skip)
                pe.matmul(out, lh, rl, start=False, stop=False, skip_group_check=skip)
                return pe.matmul(out, ll, rh, start=False, stop=last, skip_group_check=skip)

            def turn(out, src, done):
                for t in range(NT):
                    for c in range(KC):
                        last = pe.transpose(out[:, c, t * P:(t + 1) * P], src[:, t, c * P:(c + 1) * P], ident[:, :])
                last.then_inc(done, 1)

            def turn_x(g):
                pe.wait_ge(s_xn, g + 1)
                turn(XT, xn, s_xT)

            def turn_residual(g):
                pe.wait_ge(s_rn, g + 1)
                turn(GU[1], rn, s_rT)

            def q(g):
                pe.wait_ge(s_xThi, g + 1)
                pe.wait_ge(s_xTlo, g + 1)
                if isinstance(g, int) and g == 0:
                    pe.wait_ge(s_wlo, N_WQ)
                for m in range(KC):
                    for c in range(KC):
                        last = split3(Q[:, m, :],
                                      [w[:, 0, c, m * P:(m + 1) * P] for w in (whi, wlo)],
                                      [w[:, c, :] for w in (xThi, xTlo)], c == 0, c == KC - 1)
                last.then_inc(s_q, 1)

            def v(g):
                if isinstance(g, int) and g == 0:
                    pe.wait_ge(s_wlo, N_WV)
                for m in range(KC):
                    for c in range(KC):
                        split3(X[:, m, :], [w[:, 1, c, m * P:(m + 1) * P] for w in (whi, wlo)],
                               [w[:, c, :] for w in (xThi, xTlo)], m == 0 and c == 0, False, skip=True)

            def logits(g, t):
                if t == 0:
                    pe.wait_ge(s_qhi, g + 1)
                    pe.wait_ge(s_qlo, g + 1)
                    if isinstance(g, int) and g == 0:
                        pe.wait_ge(s_wlo, N_LB)
                for c in range(KC):
                    last = split3(LP[t][:, c * HC * L:(c + 1) * HC * L],
                                  [w[:, c, t * P:(t + 1) * P] for w in (qhi, qlo)],
                                  [w[:, c, :] for w in (lbhi, lblo)], True, True)
                last.then_inc(s_l, 1)

            def turn_probs(g, t):
                pe.wait_ge(s_pr, NT * g + t + 1)
                if has(g + 1):
                    pe.wait_ge(s_lg, NT * (g + 1) + t + 1)
                for j in range(J):
                    last = pe.transpose(LP[t][:, j * P:(j + 1) * P],
                                        pr[t][:, 2 * j:2 * j + 2, :].rearrange("p h l -> p (h l)"), ident[:, :])
                last.then_inc(s_pT, 1)

            def weigh(g):
                pe.wait_ge(s_pTs, NT * g + NT)
                if isinstance(g, int) and g == 0:
                    pe.wait_ge(s_lw, 16 * 2)
                for j in range(J):
                    r, m = 32 * (j % 4), j // 4
                    last = pe.matmul(X[r:r + 2 * HD, m, :], lw[:, j, :], pT[:, j, :], start=False,
                                     stop=True, skip_group_check=True)
                last.then_inc(s_a, 1)

            def attn_out(g):
                pe.wait_ge(s_ahi, g + 1)
                pe.wait_ge(s_alo, g + 1)
                if isinstance(g, int) and g == 0:
                    pe.wait_ge(s_wlo, N_BO)
                after(pe, s_dnn, g - 1)
                for t in range(NT):
                    pe.matmul(Y[:, t, :], ones[:, :], bohi[:, :], start=True, stop=False)
                    pe.matmul(Y[:, t, :], ones[:, :], bolo[:, :], start=False, stop=False)
                    for c in range(KC):
                        last = split3(Y[:, t, :], [w[:, c, t * P:(t + 1) * P] for w in (ahi, alo)],
                                      [w[:, 2, c, :] for w in (whi, wlo)], False, c == KC - 1)
                last.then_inc(s_o, 1)

            def gate_up(g, f):
                if f == 0:
                    pe.wait_ge(s_rThi, g + 1)
                    pe.wait_ge(s_rTlo, g + 1)
                if f >= 2:
                    pe.wait_ge(s_h, NC * g + f - 1)
                for u in range(2 if f < FC else 1):
                    for c in range(KC):
                        at = c * GUW + (2 * f + u) * P
                        last = split3(GU[f % 2][:, u, :], [w[:, at:at + P] for w in (fhi, flo)],
                                      [w[:, c, :] for w in (rThi, rTlo)], c == 0, c == KC - 1)
                last.then_inc(s_gu, 1)

            def down(g, f):
                if f == 0 and has(g + 1):
                    pe.wait_ge(s_an, g + 2)
                rows = P if f < FC else TAIL
                pe.wait_ge(s_hhi, NC * g + f + 1)
                pe.wait_ge(s_hlo, NC * g + f + 1)
                at = KC * GUW + f * D
                for t in range(NT):
                    last = split3(Y[:, t, :], [w[0:rows, f, t * P:(t + 1) * P] for w in (hhi, hlo)],
                                  [w[0:rows, at:at + D] for w in (fhi, flo)], f == 0 and t == 0, f == NC - 1,
                                  skip=True)
                if f == NC - 1:
                    last.then_inc(s_dn, 1)

            SPREAD = (Y[:, :, :].rearrange("p t d -> p (t d)"), GU[1][:, :, :].rearrange("p u n -> p (u n)"))
            WEIGHTS = GU[0][:, :, :].rearrange("p u n -> p (u n)")

            def spread_indices(i):
                a, w = PIECES[i]
                pe.wait_ge(s_ib, next(n for n, end in enumerate(IDX_ENDS) if a + w <= end) + 1)
                for b in range(NB):
                    k = NB * i + b
                    if k >= 2:
                        pe.wait_ge(s_rc, k - 1)
                    pe.matmul(SPREAD[k % 2][:, 0:w], spread[:, b, :, :].rearrange("p v r -> p (v r)"),
                              idxb[:, a:a + w], start=True, stop=True).then_inc(s_rp, 1)

            def look_up(i):
                w = PIECES[i][1]
                if i + 1 < len(PIECES):
                    spread_indices(i + 1)
                if i:
                    pe.wait_ge(s_fhi, i)
                    pe.wait_ge(s_flo, i)
                for q in range(STEPS):
                    pe.wait_ge(s_hot, STEPS * i + q + 1)
                    for p in range(PARTS):
                        for b in range(NB):
                            last = pe.matmul(WEIGHTS[b * RB:(b + 1) * RB, 0:w], pick[:, q, p, :],
                                             hot[:, q, b, 0:w], start=q == 0 and p == 0,
                                             stop=q == STEPS - 1 and p == PARTS - 1, skip_group_check=True)
                    last.then_inc(s_used, 1)

            def lookups(n, place):
                for i in pieces_at(n, place):
                    look_up(i)

            def body(n):
                ffn, out, tops, front = has(n), has(n + 1), has(n + 2), has(n + 3)
                lookups(n, 0)
                if ffn:
                    turn_residual(n)
                if out:
                    turn_probs(n + 1, 0)
                if ffn:
                    gate_up(n, 0)
                if out:
                    turn_probs(n + 1, 1)
                    weigh(n + 1)
                if ffn:
                    gate_up(n, 1)
                if out:
                    attn_out(n + 1)
                if ffn:
                    gate_up(n, 2)
                if tops:
                    v(n + 2)
                lookups(n, 1)
                if front:
                    turn_x(n + 3)
                lookups(n, 2)
                if ffn:
                    gate_up(n, 3)
                if front:
                    q(n + 3)
                if ffn:
                    down(n, 0)
                lookups(n, 3)
                if ffn:
                    gate_up(n, 4)
                    gate_up(n, 5)
                if front:
                    logits(n + 3, 0)
                    logits(n + 3, 1)
                if ffn:
                    down(n, 1)
                    down(n, 2)
                    down(n, 3)
                    down(n, 4)
                    down(n, 5)

            def last_body(n):
                ffn, out = has(n), has(n + 1)
                if ffn:
                    turn_residual(n)
                if out:
                    turn_probs(n + 1, 0)
                if ffn:
                    gate_up(n, 0)
                if out:
                    turn_probs(n + 1, 1)
                if ffn:
                    gate_up(n, 1)
                if out:
                    weigh(n + 1)
                    attn_out(n + 1)
                if ffn:
                    gate_up(n, 2)
                    gate_up(n, 3)
                    gate_up(n, 4)
                    gate_up(n, 5)
                    down(n, 0)
                    down(n, 1)
                    down(n, 2)
                    down(n, 3)
                    down(n, 4)
                    down(n, 5)

            pe.wait_ge(s_cst, 2)
            pe.wait_ge(s_eye, 2)
            turn_x(0)
            spread_indices(0)
            q(0)
            pe.wait_ge(s_pick, 2)
            look_up(0)
            for t in range(NT):
                logits(0, t)
            for i in range(1, EARLY):
                look_up(i)
            for n in range(-2, 0):
                body(n)
            pe.wait_ge(s_fhi, len(PIECES))
            pe.wait_ge(s_flo, len(PIECES))
            body(0)
            with pe.Fori(*LOOP) as n:
                body(n)
            body(LOOP[1])
            for n in range(LOOP[1] + 1, G + 1):
                last_body(n)

        @block.scalar
        def _(act):
            def apply(k, dst, src, g, done):
                act.wait_ge(s_nb[k], g + 1)
                for t in range(NT):
                    last = act.activation(dst[:, t, :], src(t), ACT.Identity, bias=nb[k][:, t:t + 1],
                                          scale=rstd[k][:, t:t + 1])
                last.then_inc(done, 1)

            def norm_x(g):
                apply("x", xn, lambda t: tile_of(x, g, t), g, s_xn)

            def xT(g):
                act.wait_ge(s_xT, g + 1)
                act.activation(xThi[:, :, :], XT, ACT.Copy).then_inc(s_xThi, 1)

            def q(g):
                act.wait_ge(s_q, g + 1)
                for m in range(KC):
                    last = act.activation(qhi[:, m, :], Q[:, m, :], ACT.Identity, bias=bqv[:, 0, m:m + 1])
                last.then_inc(s_qhi, 1)

            def logits(g, t):
                act.wait_ge(s_l, NT * g + t + 1)
                if has(g - 1):
                    act.wait_ge(s_marked, NT * (g - 1) + t + 1)
                    act.wait_ge(s_sh, NT * (g - 1) + t + 1)
                act.activation(lg[t][:, :, 0:L], LP[t][:, :].rearrange("p (h l) -> p h l", l=L), ACT.Copy)\
                   .then_inc(s_lg, 1)

            def exps(g, t):
                act.wait_ge(s_sh, NT * g + t + 1)
                act.activation(pr[t][:, :, :], pr[t][:, :, :], ACT.Exp, scale=HD ** -0.5).then_inc(s_ex, 1)

            def top_exps(g, t):
                act.wait_ge(s_e4, NT * g + t + 1)
                act.activation(w4[t][:, :, :], e4[t][:, :, :], ACT.Exp, scale=HD ** -0.5).then_inc(s_w4, 1)

            def probs_turned(g, t):
                act.wait_ge(s_pT, NT * g + t + 1)
                act.activation(pT[:, :, t * P:(t + 1) * P], LP[t][:, :].rearrange("p (j n) -> p j n", n=P), ACT.Copy)\
                   .then_inc(s_pTs, 1)

            def attn(g):
                act.wait_ge(s_a, g + 1)
                for m in range(KC):
                    last = act.activation(ahi[:, m, :], X[:, m, :], ACT.Identity, bias=bqv[:, 1, m:m + 1])
                last.then_inc(s_ahi, 1)

            def norm_attn(g):
                apply("a", an, lambda t: Y[:, t, :], g, s_an)

            def norm_residual(g):
                apply("r", rn, lambda t: tile_of(x, g, t), g, s_rn)

            def rT(g):
                act.wait_ge(s_rT, g + 1)
                act.activation(rThi[:, :, :], GU[1][:, :, :], ACT.Copy).then_inc(s_rThi, 1)

            def tanh(g, f):
                rows = P if f < FC else TAIL
                act.wait_ge(s_gu, NC * g + f + 1)
                act.activation(th[0:rows, f % 2, :], GU[f % 2][0:rows, 0, :], ACT.Tanh, scale=0.5).then_inc(s_th, 1)

            def h_hi(g, f):
                rows = P if f < FC else TAIL
                act.wait_ge(s_h, NC * g + f + 1)
                act.activation(hhi[0:rows, f, :], h32[0:rows, f % 2, :], ACT.Copy).then_inc(s_hhi, 1)

            def norm_down(g):
                apply("d", dn, lambda t: Y[:, t, :], g, s_dnn)

            def copy_spread(i):
                w = PIECES[i][1]
                if i == 0:
                    act.wait_ge(s_nv, NB)
                if i >= 2:
                    act.wait_ge(s_hot, STEPS * (i - 1))
                for b in range(NB):
                    k = NB * i + b
                    act.wait_ge(s_rp, k + 1)
                    bank = (Y, GU[1])[k % 2][:, :, :].rearrange("p t d -> p (t d)")
                    act.activation(rep[i % 2][:, b, 0:w], bank[:, 0:w], ACT.Identity, bias=nv[:, :]).then_inc(s_rc, 1)

            def weights_hi(i):
                a, w = PIECES[i]
                act.wait_ge(s_used, STEPS * (i + 1))
                bank = GU[0][:, :, :].rearrange("p u n -> p (u n)")
                cut = min(max(KC * GUW - a, 0), w)
                for lo, hi, scale in ((0, cut, 1.0), (cut, w, 0.5)):
                    if hi > lo:
                        last = act.activation(fhi[:, a + lo:a + hi], bank[:, lo:hi], ACT.Copy, scale=scale)
                last.then_inc(s_fhi, 1)

            def look_up(i):
                if i:
                    weights_hi(i - 1)
                if i + 1 < len(PIECES):
                    copy_spread(i + 1)
                else:
                    weights_hi(i)

            def lookups(n, place):
                for i in pieces_at(n, place):
                    look_up(i)

            def body(n):
                ffn, out, tops, front = has(n), has(n + 1), has(n + 2), has(n + 3)
                done = has(n - 1)
                lookups(n, 0)
                if ffn:
                    rT(n)
                if out:
                    probs_turned(n + 1, 0)
                    probs_turned(n + 1, 1)
                if tops:
                    top_exps(n + 2, 0)
                if ffn:
                    tanh(n, 0)
                if done:
                    norm_down(n - 1)
                if out:
                    attn(n + 1)
                if ffn:
                    h_hi(n, 0)
                lookups(n, 1)
                if tops:
                    exps(n + 2, 0)
                if ffn:
                    tanh(n, 1)
                    tanh(n, 2)
                if front:
                    norm_x(n + 3)
                if ffn:
                    h_hi(n, 1)
                if front:
                    xT(n + 3)
                if out:
                    norm_attn(n + 1)
                if ffn:
                    tanh(n, 3)
                lookups(n, 2)
                if ffn:
                    h_hi(n, 2)
                if front:
                    q(n + 3)
                lookups(n, 3)
                if tops:
                    top_exps(n + 2, 1)
                if ffn:
                    tanh(n, 4)
                    h_hi(n, 3)
                if tops:
                    exps(n + 2, 1)
                if front:
                    logits(n + 3, 0)
                if ffn:
                    tanh(n, 5)
                    h_hi(n, 4)
                    h_hi(n, 5)
                if out:
                    norm_residual(n + 1)
                if front:
                    logits(n + 3, 1)

            def last_body(n):
                ffn, out = has(n), has(n + 1)
                done = has(n - 1)
                if ffn:
                    rT(n)
                if out:
                    probs_turned(n + 1, 0)
                    probs_turned(n + 1, 1)
                if ffn:
                    tanh(n, 0)
                if done:
                    norm_down(n - 1)
                if out:
                    attn(n + 1)
                if ffn:
                    tanh(n, 1)
                    h_hi(n, 0)
                    tanh(n, 2)
                    h_hi(n, 1)
                if out:
                    norm_attn(n + 1)
                if ffn:
                    tanh(n, 3)
                    h_hi(n, 2)
                    tanh(n, 4)
                    h_hi(n, 3)
                    tanh(n, 5)
                    h_hi(n, 4)
                    h_hi(n, 5)
                if out:
                    norm_residual(n + 1)

            norm_x(0)
            act.wait_ge(s_w, 16 * 2)
            act.activation(whi[:, 0, :, :], w32[:, 0, :, :], ACT.Copy).then_inc(s_whi, 1)
            xT(0)
            copy_spread(0)
            q(0)
            act.wait_ge(s_lb, 16 * HC)
            act.activation(lbhi[:, :, :], lb32[:, :, :], ACT.Copy).then_inc(s_whi, 1)
            look_up(0)
            for t in range(NT):
                logits(0, t)
            for i in range(1, EARLY):
                look_up(i)
            act.wait_ge(s_w2, 16 * 4)
            for i in (1, 2):
                act.activation(whi[:, i, :, :], w32[:, i, :, :], ACT.Copy).then_inc(s_whi, 1)
            act.activation(bohi[:, :], bo32[:, :], ACT.Copy).then_inc(s_whi, 1)
            for n in range(-2, 1):
                body(n)
            with act.Fori(*LOOP) as n:
                body(n)
            body(LOOP[1])
            for n in range(LOOP[1] + 1, G + 1):
                last_body(n)

        @block.vector
        def _(dve):
            def held(i):
                dve.memset(spare[:, i:i + 1], 0.0)

            def stats(k, src):
                for t in range(NT):
                    last = dve.bn_stats(st[k][:, t, :], src(t))
                last.then_inc(s_st[k], 1)

            def stats_x(g):
                stats("x", lambda t: tile_of(x, g, t))

            def stats_attn(g):
                dve.wait_ge(s_o, g + 1)
                stats("a", lambda t: Y[:, t, :])

            def stats_residual(g):
                dve.wait_ge(s_x2, g + 1)
                stats("r", lambda t: tile_of(x, g, t))

            def stats_down(g):
                dve.wait_ge(s_dn, g + 1)
                stats("d", lambda t: Y[:, t, :])

            def moments(k, g):
                dve.wait_ge(s_st[k], g + 1)
                held(KINDS.index(k))
                for t in range(NT):
                    last = dve.bn_aggr(mv[k][:, t, :], st[k][:, t, :])
                last.then_inc(s_mv[k], 1)

            def var_eps(k, g):
                dve.wait_ge(s_mv[k], g + 1)
                dve.tensor_scalar(ve[k][:, :], mv[k][:, :, 1], EPS, None, ALU.add)
                dve.tensor_scalar(nm[k][:, :], mv[k][:, :, 0], -1.0, None, ALU.mult).then_inc(s_ve[k], 1)

            def low(dst, src, hi, done):
                return dve.tensor_tensor(dst, src, hi.bitcast(F32), ALU.subtract).then_inc(done, 1)

            def xT(g):
                dve.wait_ge(s_xThi, g + 1)
                low(xTlo[:, :, :], XT, xThi[:, :, :], s_xTlo)

            def biased_low(dst, src, bias, hi):
                return dve.scalar_tensor_tensor(dst, src, bias, hi.bitcast(F32), ALU.add, ALU.subtract)

            def q(g):
                dve.wait_ge(s_qhi, g + 1)
                for m in range(KC):
                    last = biased_low(qlo[:, m, :], Q[:, m, :], bqv[:, 0, m:m + 1], qhi[:, m, :])
                last.then_inc(s_qlo, 1)

            def attn(g):
                dve.wait_ge(s_ahi, g + 1)
                for m in range(KC):
                    last = biased_low(alo[:, m, :], X[:, m, :], bqv[:, 1, m:m + 1], ahi[:, m, :])
                last.then_inc(s_alo, 1)

            def rT(g):
                dve.wait_ge(s_rThi, g + 1)
                low(rTlo[:, :, :], GU[1][:, :, :], rThi[:, :, :], s_rTlo)

            def top(g, t, a=0, b=H):
                if a == 0:
                    dve.wait_ge(s_lg, NT * g + t + 1)
                    held(len(KINDS) + t)
                for h in range(a, b):
                    last = dve.max(m8[t][:, h, :], lg[t][:, h, :])
                if b == H:
                    last.then_inc(s_top, 1)

            def mark(g, t, a=0, b=H):
                for h in range(a, b):
                    last = dve.match_replace(marked[t][:, h, :], m8[t][:, h, :], lg[t][:, h, :], MARK)
                if b == H:
                    last.then_inc(s_marked, 1)

            def shift_top(g, t):
                dve.wait_ge(s_top, NT * g + t + 1)
                dve.tensor_tensor(e4[t][:, :, :], m8[t][:, :, K_TOP:2 * K_TOP],
                                  m8[t][:, :, K_TOP:K_TOP + 1].broadcast_to([P, H, K_TOP]), ALU.subtract)\
                   .then_inc(s_e4, 1)

            def sums(g, t):
                dve.wait_ge(s_w4, NT * g + t + 1)
                dve.tensor_reduce(s4[t][:, :], w4[t][:, :, :], AX_X, ALU.add).then_inc(s_s4, 1)

            def reciprocals(g, t):
                dve.wait_ge(s_s4, NT * g + t + 1)
                dve.reciprocal(r4[t][:, :], s4[t][:, :]).then_inc(s_r4, 1)

            def masks(g, t):
                dve.wait_ge(s_r4, NT * g + t + 1)
                dve.wait_ge(s_marked, NT * g + t + 1)
                dve.scalar_tensor_tensor(mk[t][:, :, :], marked[t][:, :, 0:L], MARK,
                                         r4[t][:, :].rearrange("p (h a) -> p h a", a=1).broadcast_to([P, H, L]),
                                         ALU.is_equal, ALU.mult).then_inc(s_mk, 1)

            def gate(g, f):
                rows = P if f < FC else TAIL
                dve.wait_ge(s_th, NC * g + f + 1)
                dve.scalar_tensor_tensor(ga[0:rows, f % 2, :], th[0:rows, f % 2, :], 1.0, GU[f % 2][0:rows, 0, :],
                                         ALU.add, ALU.mult).then_inc(s_ga, 1)

            def hidden(g, f):
                rows, at, u = (P, 0, 1) if f < FC else (TAIL, TU, 0)
                dve.wait_ge(s_ga, NC * g + f + 1)
                if f >= 2:
                    dve.wait_ge(s_hhi, NC * g + f - 1)
                    dve.wait_ge(s_hlo, NC * g + f - 1)
                dve.tensor_tensor(h32[0:rows, f % 2, :], ga[0:rows, f % 2, :],
                                  GU[f % 2][at:at + rows, u, :], ALU.mult).then_inc(s_h, 1)

            def one_hot(i):
                w = PIECES[i][1]
                dve.wait_ge(s_rc, NB * (i + 1))
                for q in range(STEPS):
                    k = STEPS * i + q
                    if i:
                        dve.wait_ge(s_used, k - STEPS + 1)
                    dve.tensor_scalar(hot[:, q, :, 0:w], rep[i % 2][:, :, 0:w], float(NB * q), None, ALU.is_equal)\
                       .then_inc(s_hot, 1)

            def weights_lo(i):
                a, w = PIECES[i]
                dve.wait_ge(s_fhi, i + 1)
                bank = GU[0][:, :, :].rearrange("p u n -> p (u n)")
                cut = min(max(KC * GUW - a, 0), w)
                for lo, hi, scale in ((0, cut, 1.0), (cut, w, 0.5)):
                    if hi > lo:
                        last = dve.scalar_tensor_tensor(flo[:, a + lo:a + hi], bank[:, lo:hi], scale,
                                                        fhi[:, a + lo:a + hi].bitcast(F32), ALU.mult, ALU.subtract)
                last.then_inc(s_flo, 1)

            def look_up(i):
                if i:
                    weights_lo(i - 1)
                one_hot(i)
                if i + 1 == len(PIECES):
                    weights_lo(i)

            def lookups(n, place):
                for i in pieces_at(n, place):
                    look_up(i)

            def body(n):
                ffn, out, tops, front = has(n), has(n + 1), has(n + 2), has(n + 3)
                done = has(n - 1)
                if tops:
                    top(n + 2, 0, 0, 4)
                    top(n + 2, 0, 4, 8)
                if done:
                    stats_down(n - 1)
                lookups(n, 0)
                if done:
                    moments("d", n - 1)
                if ffn:
                    rT(n)
                if tops:
                    top(n + 2, 0, 8, 12)
                if done:
                    var_eps("d", n - 1)
                if front:
                    stats_x(n + 3)
                if tops:
                    top(n + 2, 0, 12, 16)
                if front:
                    moments("x", n + 3)
                if tops:
                    shift_top(n + 2, 0)
                    mark(n + 2, 0, 0, 4)
                if ffn:
                    gate(n, 0)
                    hidden(n, 0)
                if tops:
                    mark(n + 2, 0, 4, 8)
                if out:
                    attn(n + 1)
                if tops:
                    mark(n + 2, 0, 8, 12)
                if ffn:
                    gate(n, 1)
                if front:
                    var_eps("x", n + 3)
                if tops:
                    mark(n + 2, 0, 12, 16)
                if ffn:
                    hidden(n, 1)
                if tops:
                    sums(n + 2, 0)
                if out:
                    stats_attn(n + 1)
                    moments("a", n + 1)
                    var_eps("a", n + 1)
                if tops:
                    top(n + 2, 1, 0, 4)
                lookups(n, 1)
                if tops:
                    reciprocals(n + 2, 0)
                if ffn:
                    gate(n, 2)
                if tops:
                    masks(n + 2, 0)
                if front:
                    xT(n + 3)
                lookups(n, 2)
                if tops:
                    top(n + 2, 1, 4, 8)
                if ffn:
                    hidden(n, 2)
                if tops:
                    top(n + 2, 1, 8, 12)
                    top(n + 2, 1, 12, 16)
                if ffn:
                    gate(n, 3)
                if tops:
                    shift_top(n + 2, 1)
                lookups(n, 3)
                if tops:
                    mark(n + 2, 1, 0, 4)
                if ffn:
                    hidden(n, 3)
                if front:
                    q(n + 3)
                if tops:
                    mark(n + 2, 1, 4, 8)
                if out:
                    stats_residual(n + 1)
                if tops:
                    mark(n + 2, 1, 8, 12)
                if out:
                    moments("r", n + 1)
                if tops:
                    sums(n + 2, 1)
                if out:
                    var_eps("r", n + 1)
                if ffn:
                    gate(n, 4)
                    hidden(n, 4)
                    gate(n, 5)
                    hidden(n, 5)
                if tops:
                    mark(n + 2, 1, 12, 16)
                    reciprocals(n + 2, 1)
                    masks(n + 2, 1)

            def last_body(n):
                ffn, out = has(n), has(n + 1)
                done = has(n - 1)
                if done:
                    stats_down(n - 1)
                    moments("d", n - 1)
                    var_eps("d", n - 1)
                if ffn:
                    rT(n)
                    gate(n, 0)
                    hidden(n, 0)
                if out:
                    attn(n + 1)
                if ffn:
                    gate(n, 1)
                if out:
                    stats_attn(n + 1)
                    moments("a", n + 1)
                    var_eps("a", n + 1)
                if ffn:
                    hidden(n, 1)
                    gate(n, 2)
                    hidden(n, 2)
                    gate(n, 3)
                    hidden(n, 3)
                if out:
                    stats_residual(n + 1)
                    moments("r", n + 1)
                if ffn:
                    gate(n, 4)
                if out:
                    var_eps("r", n + 1)
                if ffn:
                    hidden(n, 4)
                    gate(n, 5)
                    hidden(n, 5)

            for v in range(NB):
                dve.memset(nv[v * RB:(v + 1) * RB, :], -float(v)).then_inc(s_nv, 1)
            dve.wait_ge(s_x0, 16)
            stats_x(0)
            moments("x", 0)
            var_eps("x", 0)
            dve.wait_ge(s_eye, 1)
            for v in range(NB):
                rows = slice(v * RB, (v + 1) * RB)
                dve.tensor_copy(eye32[rows, :], eye[rows, rows]).then_inc(s_e32, 1)
            dve.wait_ge(s_v, 16)
            for v in range(NB):
                rows = slice(v * RB, (v + 1) * RB)
                dve.tensor_copy(vlut[rows, :], lut[rows, :].rearrange("p (s v) -> p v s", v=NB)[:, v, :])\
                   .then_inc(s_vl, 1)
            dve.wait_ge(s_vl, NB)
            dve.tensor_copy(parts[:, :, 0], vlut[:, :]).then_inc(s_part, 1)
            dve.wait_ge(s_part, 1)
            dve.tensor_tensor(rest[:, 0, :], vlut[:, :], parts[:, :, 0], ALU.subtract).then_inc(s_part, 1)
            dve.wait_ge(s_part, 2)
            dve.tensor_copy(parts[:, :, 1], rest[:, 0, :]).then_inc(s_part, 1)
            dve.wait_ge(s_part, 3)
            dve.tensor_tensor(rest[:, 1, :], rest[:, 0, :], parts[:, :, 1], ALU.subtract).then_inc(s_part, 1)
            dve.wait_ge(s_part, 4)
            dve.tensor_copy(parts[:, :, 2], rest[:, 1, :]).then_inc(s_part, 1)

            dve.wait_ge(s_i[0], 16 * 4)
            dve.tensor_copy(idxb[:, 0:GUW], idx[:, 0:GUW]).then_inc(s_ib, 1)
            dve.wait_ge(s_whi, N_WQ)
            low(wlo[:, 0, :, :], w32[:, 0, :, :], whi[:, 0, :, :], s_wlo)
            xT(0)
            q(0)
            one_hot(0)
            dve.wait_ge(s_whi, N_LB)
            low(lblo[:, :, :], lb32[:, :, :], lbhi[:, :, :], s_wlo)
            for i in range(1, EARLY):
                look_up(i)
            for i, n in ((1, N_WV), (2, N_WO)):
                dve.wait_ge(s_whi, n)
                low(wlo[:, i, :, :], w32[:, i, :, :], whi[:, i, :, :], s_wlo)
            dve.wait_ge(s_whi, N_BO)
            low(bolo[:, :], bo32[:, :], bohi[:, :], s_wlo)
            dve.wait_ge(s_x1, 16)
            body(-2)
            dve.wait_ge(s_xr, 16 * 2)
            body(-1)
            body(0)
            with dve.Fori(*LOOP) as n:
                body(n)
            body(LOOP[1])
            for n in range(LOOP[1] + 1, G + 1):
                last_body(n)

        @block.gpsimd
        def _(pool):
            pool.memset(lb32[:, :, :], 0.0)
            pool.memset(lw[:, :, :], 0.0).then_inc(s_pad, 1)
            for c in range(KC):
                pool.memset(idx[:, c * GUW + 2 * FC * P:(c + 1) * GUW], 0)
            pool.memset(idx[:, KC * GUW + FC * D:WALL], 0).then_inc(s_pad, 2)
            pool.memset(half[:, :], -0.5)
            pool.memset(ones[:, :].bitcast(F32), 1.0).then_inc(s_out, 16)
            for t in range(NT):
                pool.memset(lg[t][:, :, L:LROW], SENTINEL)
            pool.memset(ident[:, :], 0.0).then_inc(s_cst, 1)
            pool.wait_ge(s_cst, 1)
            pool.affine_select(out=ident[:, :], in_=ident[:, :], compare_op=ALU.not_equal, fill=1.0,
                               base=0, pattern=[[-1, P]], channel_multiplier=1).then_inc(s_cst, 1)
            pool.wait_ge(s_cst, 2)

            def rstds(k, g):
                pool.wait_ge(s_ve[k], g + 1)
                pool.tensor_tensor(rstd[k][:, :], ve[k][:, :], half[:, :], ALU.pow).then_inc(s_rs[k], 1)
                pool.wait_ge(s_rs[k], g + 1)
                pool.tensor_tensor(nb[k][:, :], nm[k][:, :], rstd[k][:, :], ALU.mult).then_inc(s_nb[k], 1)

            def rows_of(g):
                return x[:, NT * g:NT * g + NT, :] if isinstance(g, int) else x[:, bass.ds(NT * g, NT), :]

            def residual(g):
                pool.wait_ge(s_an, g + 1)
                pool.tensor_tensor(rows_of(g), an[:, :, :], rows_of(g), ALU.add).then_inc(s_x2, 1)

            def shift(g, t):
                pool.wait_ge(s_top, NT * g + t + 1)
                if has(g - 1):
                    pool.wait_ge(s_pT, NT * (g - 1) + t + 1)
                pool.tensor_tensor(pr[t][:, :, :], lg[t][:, :, 0:L],
                                   m8[t][:, :, K_TOP:K_TOP + 1].broadcast_to([P, H, L]), ALU.subtract)\
                    .then_inc(s_sh, 1)

            def probs(g, t):
                pool.wait_ge(s_ex, NT * g + t + 1)
                pool.wait_ge(s_mk, NT * g + t + 1)
                pool.tensor_tensor(pr[t][:, :, :], pr[t][:, :, :], mk[t][:, :, :], ALU.mult).then_inc(s_pr, 1)

            def h_lo(g, f):
                rows = P if f < FC else TAIL
                pool.wait_ge(s_hhi, NC * g + f + 1)
                pool.tensor_tensor(hlo[0:rows, f, :], h32[0:rows, f % 2, :], hhi[0:rows, f, :].bitcast(F32),
                                   ALU.subtract).then_inc(s_hlo, 1)

            def output(g):
                pool.wait_ge(s_dnn, g + 1)
                pool.wait_ge(s_out, 16 * (g + 1))
                pool.tensor_tensor(y[:, :, :], dn[:, :, :], rows_of(g), ALU.add).then_inc(s_y, 1)

            def body(n):
                ffn, out, tops, front = has(n), has(n + 1), has(n + 2), has(n + 3)
                done = has(n - 1)
                if done:
                    rstds("d", n - 1)
                if tops:
                    shift(n + 2, 0)
                if front:
                    rstds("x", n + 3)
                if ffn:
                    h_lo(n, 0)
                if out:
                    rstds("a", n + 1)
                if ffn:
                    h_lo(n, 1)
                if out:
                    residual(n + 1)
                if ffn:
                    h_lo(n, 2)
                if tops:
                    shift(n + 2, 1)
                if done:
                    output(n - 1)
                if ffn:
                    h_lo(n, 3)
                if out:
                    rstds("r", n + 1)
                if ffn:
                    h_lo(n, 4)
                    h_lo(n, 5)
                if tops:
                    probs(n + 2, 0)
                    probs(n + 2, 1)

            def last_body(n):
                ffn, out = has(n), has(n + 1)
                done = has(n - 1)
                if done:
                    rstds("d", n - 1)
                if ffn:
                    h_lo(n, 0)
                if done:
                    output(n - 1)
                if out:
                    rstds("a", n + 1)
                if ffn:
                    h_lo(n, 1)
                if out:
                    residual(n + 1)
                if ffn:
                    h_lo(n, 2)
                    h_lo(n, 3)
                if out:
                    rstds("r", n + 1)
                if ffn:
                    h_lo(n, 4)
                    h_lo(n, 5)

            pool.tensor_copy(eye[:, :], ident[:, :]).then_inc(s_eye, 1)
            pool.wait_ge(s_eye, 1)
            pool.tensor_copy(spread[:, :, :, :],
                             eye[:, :].rearrange("p (b a r) -> p b a r", b=NB, a=1).broadcast_to([P, NB, NB, RB]))\
                .then_inc(s_eye, 1)
            pool.wait_ge(s_eye, 2)
            rstds("x", 0)
            def index_values(i):
                pool.wait_ge(s_i[i], 16 * (4 if i < KC else 2))
                at = IDX_ENDS[i - 1]
                pool.tensor_copy(idxb[:, at:IDX_ENDS[i]], idx[:, at:IDX_ENDS[i]]).then_inc(s_ib, 1)

            pool.wait_ge(s_part, 5)
            pool.wait_ge(s_e32, NB)
            pool.tensor_tensor(pick[:, :, :, :].rearrange("p q t r -> p (q t) r"),
                               eye32[:, :].rearrange("p (a r) -> p a r", a=1).broadcast_to([P, STEPS * PARTS, RB]),
                               parts[:, :, :].rearrange("p q (t a) -> p (q t) a", a=1)
                               .broadcast_to([P, STEPS * PARTS, RB]), ALU.mult).then_inc(s_pick, 2)
            pool.wait_ge(s_ib, 1)
            index_values(1)
            index_values(2)
            for n in range(-2, LOOP[0]):
                body(n)
            with pool.Fori(*LOOP) as n:
                body(n)
            body(LOOP[1])
            for n in range(LOOP[1] + 1, G + 1):
                last_body(n)


def kernel(**inputs):
    import numpy as np
    import concourse.bacc as bacc
    from concourse.bass_utils import run_bass_kernel_spmd

    def a(name):
        return np.asarray(inputs[name])

    lay = np.ascontiguousarray
    arrays = {
        "x_in": lay(a("L0_attn_hidden_states")[0]),
        "wq_in": lay(a("L0_attn_Wq").T), "bq_in": lay(a("L0_attn_bq").reshape(KC, P).T),
        "wv_in": lay(a("L0_attn_Wv").T), "bv_in": lay(a("L0_attn_bv").reshape(KC, P).T),
        "wo_in": lay(a("L0_attn_Wo").T), "bo_in": lay(a("L0_attn_bo")),
        "lat_in": lay(a("L0_attn_latent_keys")), "latT_in": lay(a("L0_attn_latent_keys").T),
        "lut_in": lay(a("L0_ffn_lut")),
        "gate_in": lay(a("L0_ffn_gate_idx").T), "up_in": lay(a("L0_ffn_up_idx").T),
        "down_in": lay(a("L0_ffn_down_idx").T),
    }
    nc = bacc.Bacc("TRN2", target_bir_lowering=False, num_devices=1)
    args = [nc.dram_tensor(n, v.shape, mybir.dt.from_np(v.dtype), kind="ExternalInput").ap() for n, v in arrays.items()]
    out = nc.dram_tensor("out", (T, D), F32, kind="ExternalOutput").ap()
    build(nc, *args, out)
    r = run_bass_kernel_spmd(nc, [arrays], core_ids=[0])
    return r.results[0]["out"].reshape(1, T, D)
```
